# Optimizing a Trainium2 kernel written in Bass

```python
import numpy as np
import jax
import jax.numpy as jnp

def _softmax(x, axis=-1):
    return jax.nn.softmax(x, axis=axis)

def _gelu(x):
    return jax.nn.gelu(x, approximate=True)

def _silu(x):
    return jax.nn.silu(x)

def _sigmoid(x):
    return jax.nn.sigmoid(x)

def _layernorm(x, axis=-1, eps=1e-05):
    m = jnp.mean(x, axis=axis, keepdims=True)
    v = jnp.var(x, axis=axis, keepdims=True)
    return (x - m) / jnp.sqrt(v + eps)

def _scatter_add(tgt, idx, src, axis=0):
    return tgt.at[idx].add(src)

def _segment_sum(src, seg, n):
    return jax.ops.segment_sum(src, seg, n)
kernel_name = 'mk_gnn_preln_d2_gnn_r16_3212a0'

def setup_inputs(seed: int=0):
    np.random.seed(seed)
    _w = jnp.asarray

    def _rec_inputs():
        import jax
        import jax.numpy as jnp
        _gk = jax.random.key(seed)
        x = 1.712e-05 + 0.1 * jax.random.normal(jax.random.fold_in(_gk, 1), (6250, 16), jnp.float32)
        _s = jax.random.randint(jax.random.fold_in(_gk, 2), (100000,), 0, 6250, jnp.int32)
        _d = jax.random.randint(jax.random.fold_in(_gk, 3), (100000,), 0, 6250, jnp.int32)
        _loop = jnp.arange(6250, dtype=jnp.int32)
        src = jnp.concatenate([_s, _d, _loop])
        dst = jnp.concatenate([_d, _s, _loop])
        _o = jnp.argsort(dst, stable=True)
        src = src[_o]
        dst = dst[_o]
        edge_attr_16 = -3.57403e-05 + 0.999761 * jax.random.normal(jax.random.fold_in(_gk, 13), (206250, 16), jnp.float32)
        edge_type_230 = jax.random.randint(jax.random.fold_in(_gk, 14), (206250,), 0, 230, jnp.int32)
        return (x, src, dst, edge_attr_16, edge_type_230)
    x, src, dst, edge_attr_16, edge_type_230 = _rec_inputs()

    def _L0_gnn_setup():
        import jax, jax.numpy as jnp
        import numpy as np
        C = 0.01
        EPS = 1e-06
        MIN_NORM = 1e-10
        BALL_EPS = 1e-05

        def _norm(x):
            return jnp.sqrt(jnp.clip(jnp.sum(x * x, axis=-1, keepdims=True), MIN_NORM))

        def log_map_zero(x, c):
            sc = jnp.sqrt(c)
            n = _norm(x)
            return jnp.arctanh(jnp.clip(sc * n, -1.0 + BALL_EPS, 1.0 - BALL_EPS)) * x / (sc * n)

        def exp_map_zero(v, c):
            sc = jnp.sqrt(c)
            n = _norm(v)
            return jnp.tanh(sc * n) * v / (sc * n)

        def project_to_ball(x, c):
            n = _norm(x)
            maxn = (1.0 - BALL_EPS) / jnp.sqrt(c)
            return jnp.where(n > maxn, x * (maxn / n), x)

        def mobius_add(x, y, c):
            x2 = jnp.sum(x * x, axis=-1, keepdims=True)
            y2 = jnp.sum(y * y, axis=-1, keepdims=True)
            xy = jnp.sum(x * y, axis=-1, keepdims=True)
            num = (1.0 + 2.0 * c * xy + c * y2) * x + (1.0 - c * x2) * y
            den = 1.0 + 2.0 * c * xy + c * c * x2 * y2
            return num / jnp.clip(den, MIN_NORM)
        N, E, R, D = (3125, 25000, 230, 16)
        key = jax.random.key(seed)
        ks = jax.random.split(key, 8)
        h_hyper = project_to_ball(0.1 * jax.random.normal(ks[0], (N, D), dtype=jnp.float32), C)
        node_norm = jax.random.uniform(ks[1], (N, 1), dtype=jnp.float32)
        xav = float(np.sqrt(2.0 / (D + D)))
        rel_weight = xav * jax.random.normal(ks[2], (R, D, D), dtype=jnp.float32)
        loop_weight = xav * jax.random.normal(ks[3], (D, D), dtype=jnp.float32)
        rel_emb = 0.1 * jax.random.normal(ks[4], (R, D), dtype=jnp.float32)
        src = jax.random.randint(ks[5], (E,), 0, N, dtype=jnp.int32)
        dst = jax.random.randint(ks[6], (E,), 0, N, dtype=jnp.int32)
        etype = jax.random.randint(ks[7], (E,), 0, R, dtype=jnp.int32)
        return {'h_hyper': h_hyper, 'node_norm': node_norm, 'rel_weight': rel_weight, 'loop_weight': loop_weight, 'rel_emb': rel_emb, 'src': src, 'dst': dst, 'etype': etype}
    _L0_gnn_all = _L0_gnn_setup()
    _L0_gnn_in = {k: v for k, v in _L0_gnn_all.items() if k in ('rel_weight', 'loop_weight', 'rel_emb')}
    del _L0_gnn_all

    def _L1_gnn_setup():
        import jax, jax.numpy as jnp
        import numpy as np
        N_NODES = 1875
        N_EDGES = 18750
        IN_FEATS = 16
        OUT_FEATS = 16
        EDGE_DIM = 16
        key = jax.random.key(seed)
        ks = jax.random.split(key, 8)
        feat = jax.random.normal(ks[0], (N_NODES, IN_FEATS), dtype=jnp.float32)
        efeat = jax.random.normal(ks[1], (N_EDGES, EDGE_DIM), dtype=jnp.float32)
        W_msg = jax.random.normal(ks[2], (EDGE_DIM, IN_FEATS * OUT_FEATS), dtype=jnp.float32) * 0.1
        b_msg = jnp.zeros((IN_FEATS * OUT_FEATS,), dtype=jnp.float32)
        W_attn = jax.random.normal(ks[3], (EDGE_DIM, IN_FEATS * OUT_FEATS), dtype=jnp.float32) * 0.1
        b_attn = jnp.zeros((IN_FEATS * OUT_FEATS,), dtype=jnp.float32)
        src = jax.random.randint(ks[4], (N_EDGES,), 0, N_NODES, dtype=jnp.int32)
        dst = jax.random.randint(ks[5], (N_EDGES,), 0, N_NODES, dtype=jnp.int32)
        return {'feat': feat, 'efeat': efeat, 'W_msg': W_msg, 'b_msg': b_msg, 'W_attn': W_attn, 'b_attn': b_attn, 'src': src, 'dst': dst}
    _L1_gnn_all = _L1_gnn_setup()
    _L1_gnn_in = {k: v for k, v in _L1_gnn_all.items() if k in ('W_msg', 'b_msg', 'W_attn', 'b_attn')}
    del _L1_gnn_all
    return {'x': x, 'src': src, 'dst': dst, 'edge_attr_16': edge_attr_16, 'edge_type_230': edge_type_230, 'L0_gnn_rel_weight': _L0_gnn_in['rel_weight'], 'L0_gnn_loop_weight': _L0_gnn_in['loop_weight'], 'L0_gnn_rel_emb': _L0_gnn_in['rel_emb'], 'L1_gnn_W_msg': _L1_gnn_in['W_msg'], 'L1_gnn_b_msg': _L1_gnn_in['b_msg'], 'L1_gnn_W_attn': _L1_gnn_in['W_attn'], 'L1_gnn_b_attn': _L1_gnn_in['b_attn']}

def reference(x, src, dst, edge_attr_16, edge_type_230, L0_gnn_rel_weight, L0_gnn_loop_weight, L0_gnn_rel_emb, L1_gnn_W_msg, L1_gnn_b_msg, L1_gnn_W_attn, L1_gnn_b_attn):
    import jax
    import jax.numpy as jnp

    def _L0_gnn_ref(h_hyper, node_norm, rel_weight, loop_weight, rel_emb, src, dst, etype):
        import jax, jax.numpy as jnp
        import numpy as np
        C = 0.01
        EPS = 1e-06
        MIN_NORM = 1e-10
        BALL_EPS = 1e-05

        def _norm(x):
            return jnp.sqrt(jnp.clip(jnp.sum(x * x, axis=-1, keepdims=True), MIN_NORM))

        def log_map_zero(x, c):
            sc = jnp.sqrt(c)
            n = _norm(x)
            return jnp.arctanh(jnp.clip(sc * n, -1.0 + BALL_EPS, 1.0 - BALL_EPS)) * x / (sc * n)

        def exp_map_zero(v, c):
            sc = jnp.sqrt(c)
            n = _norm(v)
            return jnp.tanh(sc * n) * v / (sc * n)

        def project_to_ball(x, c):
            n = _norm(x)
            maxn = (1.0 - BALL_EPS) / jnp.sqrt(c)
            return jnp.where(n > maxn, x * (maxn / n), x)

        def mobius_add(x, y, c):
            x2 = jnp.sum(x * x, axis=-1, keepdims=True)
            y2 = jnp.sum(y * y, axis=-1, keepdims=True)
            xy = jnp.sum(x * y, axis=-1, keepdims=True)
            num = (1.0 + 2.0 * c * xy + c * y2) * x + (1.0 - c * x2) * y
            den = 1.0 + 2.0 * c * xy + c * c * x2 * y2
            return num / jnp.clip(den, MIN_NORM)
        c = C
        N = h_hyper.shape[0]
        h_tan = log_map_zero(h_hyper, c)
        msg_tan = jnp.einsum('ei,eio->eo', h_tan[src], rel_weight[etype])
        msg_tan = msg_tan + rel_emb[etype]
        msg = exp_map_zero(msg_tan, c)
        en = node_norm[dst, 0]
        norm_sum = jax.ops.segment_sum(en, dst, num_segments=N)
        w = en / (norm_sum[dst] + EPS)
        lam = 2.0 / (1.0 - c * jnp.sum(msg * msg, axis=-1) + EPS)
        wl = w * lam
        numer = jax.ops.segment_sum(wl[:, None] * msg, dst, num_segments=N)
        denom = jax.ops.segment_sum(wl, dst, num_segments=N) + EPS
        h_agg = project_to_ball(numer / denom[:, None], c)
        loop_hyp = exp_map_zero(h_tan @ loop_weight, c)
        h_new = mobius_add(h_agg, loop_hyp, c)
        return h_new

    def _L1_gnn_ref(feat, efeat, W_msg, b_msg, W_attn, b_attn, src, dst):
        import jax, jax.numpy as jnp
        import numpy as np
        N_NODES = 1875
        N_EDGES = 18750
        IN_FEATS = 16
        OUT_FEATS = 16
        EDGE_DIM = 16
        N, in_f = feat.shape
        E = efeat.shape[0]
        w_m = (efeat @ W_msg + b_msg).reshape(E, in_f, -1)
        w_a = (efeat @ W_attn + b_attn).reshape(E, in_f, -1)
        h_src = feat[src][:, :, None]
        e1 = w_m * h_src
        e2 = w_a * h_src
        seg_max = jax.ops.segment_max(e2, dst, num_segments=N)
        ex = jnp.exp(e2 - seg_max[dst])
        denom = jax.ops.segment_sum(ex, dst, num_segments=N)
        attn = ex / denom[dst]
        ft = jax.ops.segment_sum(e1 * attn, dst, num_segments=N)
        return ft.sum(axis=1)
    deg = jnp.maximum(jax.ops.segment_sum(jnp.ones(dst.shape, jnp.float32), dst, num_segments=6250), 1.0)
    deg_isqrt = deg ** (-0.5)
    h = jnp.maximum(_layernorm(x, axis=-1), 0.0)
    x = x + _L0_gnn_ref(h, deg_isqrt[:, None], L0_gnn_rel_weight, L0_gnn_loop_weight, L0_gnn_rel_emb, src, dst, edge_type_230)
    h = jnp.maximum(_layernorm(x, axis=-1), 0.0)
    x = x + _L1_gnn_ref(h, edge_attr_16, L1_gnn_W_msg, L1_gnn_b_msg, L1_gnn_W_attn, L1_gnn_b_attn, src, dst)
    return x

_drawn_inputs = setup_inputs


def setup_inputs(seed=0):
    import zlib

    import numpy as np

    out = dict(_drawn_inputs(seed))
    spreads = {'L1_gnn_b_msg': (0.0, 0.1), 'L1_gnn_b_attn': (0.0, 0.1)}
    factors = {}
    for name, (base, spread) in spreads.items():
        noise = np.random.default_rng([zlib.crc32(name.encode()), seed]).standard_normal(out[name].shape)
        drawn = base * np.exp(spread * noise) if base else spread * noise
        out[name] = jnp.asarray(drawn.astype(out[name].dtype))
    for name, factor in factors.items():
        out[name] = (out[name] * factor).astype(out[name].dtype)
    return out
```

```python
from contextlib import ExitStack

import concourse.bass as bass
from concourse import mybir

F32 = mybir.dt.float32
BF16 = mybir.dt.bfloat16
I32 = mybir.dt.int32
I16 = mybir.dt.int16
U32 = mybir.dt.uint32
ALU = mybir.AluOpType
ACT = mybir.ActivationFunctionType
AX = mybir.AxisListType
ds = bass.ds

N, D, E, R = 6250, 16, 206250, 230
PN = 125
C = N // PN
IO = D * D
BLK = 6
NBW = 8
S = BLK * NBW
MINB = 3
NW = 4608
KE = D + 2
RO = R * D
PIECE = RO // 8
ROW = 110
NROW = E // ROW
RPP = NROW // PN
EPP = E // PN
INFO = 2 * D + 4

BIG = 2.0 ** 120
CURV = 0.01
SQC = 0.1
EPS = 1e-6
MIN_NORM = 1e-10
BALL = 1e-5
LN_EPS = 1e-5


def build(nc, x, src, dst, efeat, etype, relw, loopw, relemb, wmsg, bmsg, wattn, battn, out, scratch):
    table_d, srcp_d, pairp_d, efp_d, h2_d, first_d, key_d, info_d = scratch
    ctx = ExitStack()
    with ctx:
        def sb(name, shape, dt=F32):
            return ctx.enter_context(nc.sbuf_tensor(name, shape, dt))

        def sem(name):
            return ctx.enter_context(nc.semaphore(name))

        arena = sb("arena", [128, 2 * S * IO])

        def at(off, n, p=PN, dt=F32):
            v = arena[0:p, off:off + n]
            return v if dt is F32 else v.bitcast(dt)

        score = arena[0:PN, :].rearrange("p (q s c) -> p q s c", q=2, c=IO)
        tbl = at(0, 2 * RO).rearrange("p (q n) -> p q n", q=2)
        o = 2 * RO
        firstrow = at(o, NROW)
        dstblk = at(o + NROW, (C + 1) * ROW, dt=I32).rearrange("p (c w) -> p c w", w=ROW)
        dst_sb = at(o + NROW, EPP, dt=I32)
        keyrow = at(o, N)
        junk = at(o + NROW + (C + 1) * ROW, N)
        less = junk[:, 0:(C + 1) * ROW].rearrange("p (c w) -> p c w", w=ROW)
        winint, winpos = at(o, NW, C, I32), at(o, NW, C)
        winhot, winrel = at(o + NW, NW, C), at(o + 2 * NW, NW, C)
        rec = at(22700, C * INFO).rearrange("p (c w) -> p c w", w=INFO)

        def tmp(i):
            return at(o + NROW + (C + 1) * ROW + i * C * D, C * D).rearrange("p (c d) -> p c d", d=D)

        stage = sb("stage", [128, 6960])
        prod = stage[0:PN, 0:2 * BLK * IO]
        o2 = 2 * BLK * IO
        ef18 = stage[0:PN, o2:o2 + 2 * S * KE].rearrange("p (q s k) -> p q s k", q=2, k=KE)
        o2 += 2 * S * KE
        efT = stage[0:BLK * KE, o2:o2 + 2 * NBW * 128].rearrange("k (q b n) -> k q b n", q=2, n=128)
        relW = stage[0:64, 0:RO + D]
        htan32 = stage[0:PN, 3700:3700 + C * 32].rearrange("p (c k) -> p c k", k=32)
        numer = stage[0:PN, 0:(C + 1) * D].rearrange("p (c d) -> p c d", d=D)

        work = sb("work", [128, BLK * IO + 9 * IO])
        hT = work[0:64, 0:(C // 2) * 128].rearrange("k (m n) -> k m n", n=128)
        sq = work[0:PN, 0:S * D].rearrange("p (s d) -> p s d", d=D)
        sl = work[0:PN, S * D:S * D + 6 * S].rearrange("p (j s) -> p j s", s=S)
        macc = work[0:PN, 0:BLK * IO].rearrange("p (s c) -> p s c", c=IO)

        def col256(j, n=1):
            return work[0:PN, BLK * IO + j * IO:BLK * IO + (j + n) * IO]

        mred, mold, cfac, ratio = col256(0), col256(1), col256(2), col256(3)
        total = col256(4, 2).rearrange("p (a c) -> p a c", a=2)
        mnew = col256(6, 2).rearrange("p (q c) -> p q c", q=2)
        diff = col256(8)

        gath = sb("gath", [PN, 2, S, D])
        efraw = sb("efraw", [PN, 2, max(S * D, EPP // 2)])
        src_sb = stage[0:PN, 5300:5300 + EPP].bitcast(I32)
        et_sb = efraw[:, :, :].rearrange("p q n -> p (q n)")[:, 0:EPP].bitcast(I32)
        pair_sb = et_sb
        wA = sb("wA", [BLK * KE, BLK, IO])
        wM = sb("wM", [BLK * KE, BLK, IO])
        info = sb("info", [PN, C + 1, INFO])
        xnew = sb("xnew", [PN, C + 1, D])
        h2 = sb("h2", [PN, C, D])
        lamsum = sb("lamsum", [PN, C + 1])
        hst = sb("hst", [64, PN])
        tabgn, tabs = sb("tabgn", [PN, NW], I16), sb("tabs", [PN, NW], I16)
        ident = sb("ident", [128, 128])
        tri = sb("tri", [C, C])
        ones = sb("ones", [C, PN])
        zero = sb("zero", [1, 512], BF16)
        negbig = sb("negbig", [1, IO])
        pad1 = sb("pad1", [1, D])
        padrow = gath[0:1, 0, :, :].rearrange("p s d -> p (s d)")
        nodei = sb("nodei", [PN, C + 1], I32)
        nodeid = sb("nodeid", [PN, C + 1])
        iotai = sb("iotai", [PN, S], I32)
        iotaf = sb("iotaf", [PN, S])
        firsts = sb("firsts", [PN, RPP])
        cnt = sb("cnt", [PN, C + 1])
        rowi = sb("rowi", [PN, C + 1], I32)
        start0 = sb("start0", [PN, C + 1])
        key = sb("key", [PN, C])
        rank = sb("rank", [PN, C])
        ranki = sb("ranki", [PN, C], I32)
        nidx = sb("nidx", [PN, C + 1], I32)
        col = sb("col", [C, 8])
        lhs = sb("lhs", [C, 3, PN])
        npairf = sb("npairf", [PN, 1])
        npair = sb("npair", [PN, 1], I32)
        nrm = sb("nrm", [PN, 8, C])
        bstf = sb("bstf", [PN, 2])
        bst = sb("bst", [PN, 2], I32)
        rem = sb("rem", [PN, 2])
        keep = sb("keep", [PN, 2])
        keepbig = sb("keepbig", [PN, 2])
        blkidx = sb("blkidx", [PN, 2, S], I32)
        hidx = sb("hidx", [PN, 2, S], I32)
        valid = sb("valid", [PN, 2, S])
        wvt = work[0:PN, 0:1024].rearrange("p (a n) -> p a n", a=2)
        valid2 = sb("valid2", [PN, S])
        npad = sb("npad", [PN, 1])
        lsum = sb("lsum", [PN, 1])
        nsum = sb("nsum", [PN, D])
        orow = sb("orow", [PN, 2, D])
        oidx = sb("oidx", [PN, 2], I32)
        ft = sb("ft", [PN, D])

        psW = ctx.enter_context(nc.psum_tensor("psW", [128, 2, 1024], F32))
        psS = ctx.enter_context(nc.psum_tensor("psS", [128, 512], F32))
        psT = ctx.enter_context(nc.psum_tensor("psT", [128, 12, 128], F32))

        names = ("x_in dst_in edges_in relw_in wts_in wzero const node_tmp var_ready std_ready htan_ready hT_ps hT_sb "
                 "tbl_ps tbl_psfree tbl_sb tbl_out0 tbl_out1 firsts_ready firsts_dram firstrow_in rows_ready rows_in "
                 "key_ready key_dram keyrow_in pair_ready pair_out srcp_out efp_out pad_out "
                 "loop_ready hst_sb pe_free rec_ready info_dram info_in deg_T deg_red plan_col plan_ps win_ready win_ps win_psfree "
                 "passed win_iota loop_n loop_t loop_norm tab_done "
                 "bst_ready blk_in tg0 tg1 l0_math n2_ready th_ready hnorm hnorm_out x2_var x2_std h2_ready h2_out "
                 "bst1_ready src_in ef_in idx_ready hg0 hg1 h_free efT_ps efT_sb w_ready w_free d_ready c_ready "
                 "sub_done exp_done q_ready q_free sum_done sum_read fin out_done init credit").split()
        m = {n: sem("s_" + n) for n in names}
        tgath, hgath = (m["tg0"], m["tg1"]), (m["hg0"], m["hg1"])

        block = ctx.enter_context(nc.Block())

        def bc(v, n):
            return v.unsqueeze(len(v.shape)).to_broadcast(list(v.shape) + [n])

        def window(eng, k):
            v = eng.value_load(tabgn[0:1, ds(k, 1)], min_val=0, max_val=C * NBW + NBW - 1)
            return v // NBW, v % NBW + 1

        @block.sync
        def _(sp):
            sp.dma_start(rec[:, :, 0:D], x.rearrange("(p c) d -> p c d", p=PN)).then_inc(m["x_in"], 16)
            sp.dma_start(dst_sb, dst.rearrange("(p e) -> p e", p=PN)).then_inc(m["dst_in"], 16)
            sp.wait_ge(m["wzero"], 1)
            for j in range(2):
                p = 32 * j
                sp.dma_start(relW[p:p + D, 0:RO].rearrange("i (r o) -> i r o", o=D),
                             relw.rearrange("r i o -> i r o")).then_inc(m["relw_in"], 16)
                sp.dma_start(relW[p + D:p + D + 1, 0:RO], relemb.rearrange("(a r) o -> a (r o)", a=1)).then_inc(m["relw_in"], 16)
                sp.dma_start(relW[p:p + D, RO:RO + D], loopw).then_inc(m["relw_in"], 16)
            sp.dma_start(src_sb, src.rearrange("(p e) -> p e", p=PN)).then_inc(m["edges_in"], 16)
            sp.dma_start(et_sb, etype.rearrange("(p e) -> p e", p=PN)).then_inc(m["edges_in"], 16)
            sp.dma_start(srcp_d[0:E].rearrange("(a b) -> a b", b=250), src.rearrange("(a b) -> a b", b=250)).then_inc(m["srcp_out"], 16)
            for j in range(BLK):
                p = KE * j
                for w, wt, bias in ((wA, wattn, battn), (wM, wmsg, bmsg)):
                    sp.dma_start(w[p:p + D, j, :], wt).then_inc(m["wts_in"], 16)
                    sp.dma_start(w[p + D:p + D + 1, j, :], bias.rearrange("(a c) -> a c", a=1)).then_inc(m["wts_in"], 16)
                sp.dma_start(wA[p + D + 1:p + D + 2, j, :], negbig[:]).then_inc(m["wts_in"], 16)
            sp.dma_start(srcp_d[E:E + S].rearrange("(a b) -> a b", a=1), padrow[:, 0:S].bitcast(I32)).then_inc(m["pad_out"], 16)
            sp.dma_start(pairp_d[E:E + S].rearrange("(a b) -> a b", a=1), padrow[:, 0:S].bitcast(I32)).then_inc(m["pad_out"], 16)
            sp.dma_start(efp_d[E * D:(E + S) * D].rearrange("(a b) -> a b", a=1), padrow).then_inc(m["pad_out"], 16)
            sp.dma_start(h2_d[N:N + 1, :], pad1[:]).then_inc(m["pad_out"], 16)
            rows = table_d.rearrange("(p c r) d -> p c (r d)", p=PN, c=C)
            with sp.Fori(0, C // 2) as t:
                for j in range(2):
                    sp.wait_ge(m["tbl_sb"], t * 8 + (4 * j + 4 + 2))
                    for a, b in ((0, 112), (112, PN)):
                        sp.dma_start(rows[a:b, ds(2 * t + j, 1), :].rearrange("p a n -> p (a n)"),
                                     tbl[a:b, j, :]).then_inc(m[f"tbl_out{j}"], 16)
            sp.dma_start(efp_d[0:E * D].rearrange("(a b) -> a b", b=1375),
                         efeat.rearrange("e d -> (e d)").rearrange("(a b) -> a b", b=1375)).then_inc(m["efp_out"], 16)
            sp.wait_ge(m["efp_out"], 16)

        @block.gpsimd
        def _(pool):
            pool.memset(ident[:], 0.0).then_inc(m["init"], 1)
            pool.memset(tri[:], 1.0).then_inc(m["init"], 1)
            pool.iota(nodei[:], [[1, C + 1]], base=0, channel_multiplier=C).then_inc(m["init"], 1)
            pool.iota(iotai[:], [[1, S]], base=0, channel_multiplier=0).then_inc(m["init"], 1)
            pool.wait_ge(m["init"], 4)
            pool.affine_select(out=ident[:], in_=ident[:], compare_op=ALU.not_equal, fill=1.0, base=0,
                               pattern=[[-1, 128]], channel_multiplier=1).then_inc(m["const"], 1)
            pool.affine_select(out=tri[:], in_=tri[:], compare_op=ALU.is_ge, fill=0.0, base=0,
                               pattern=[[1, C]], channel_multiplier=-1).then_inc(m["const"], 1)
            pool.wait_ge(m["firsts_ready"], 1)
            pool.dma_start(first_d.rearrange("(p c) -> p c", p=PN), firsts[:]).then_inc(m["firsts_dram"], 16)
            pool.wait_ge(m["firsts_dram"], 16)
            pool.dma_start(firstrow, first_d.rearrange("(a c) -> a c", a=1).to_broadcast([PN, NROW])).then_inc(m["firstrow_in"], 16)
            pool.wait_ge(m["rows_ready"], 1)
            for c in range(C + 1):
                pool.indirect_dma_start(out=dstblk[:, c, :], out_offset=None, in_=dst.rearrange("(r w) -> r w", w=ROW),
                                        in_offset=bass.IndirectOffsetOnAxis(ap=rowi[:, c:c + 1].bitcast(U32), axis=0)).then_inc(m["rows_in"], 16)
            pool.wait_ge(m["pair_ready"], 1)
            pool.dma_start(pairp_d[0:E].rearrange("(p e) -> p e", p=PN), pair_sb).then_inc(m["pair_out"], 16)
            pool.wait_ge(m["key_ready"], 1)
            pool.dma_start(key_d.rearrange("(p c) -> p c", p=PN), key[:]).then_inc(m["key_dram"], 16)
            pool.wait_ge(m["key_dram"], 16)
            pool.dma_start(keyrow, key_d.rearrange("(a c) -> a c", a=1).to_broadcast([PN, N])).then_inc(m["keyrow_in"], 16)
            pool.wait_ge(m["rec_ready"], 1)
            for c in range(C):
                pool.indirect_dma_start(out=info_d, out_offset=bass.IndirectOffsetOnAxis(ap=ranki[:, c:c + 1].bitcast(U32), axis=0),
                                        in_=rec[:, c, :], in_offset=None).then_inc(m["info_dram"], 16)
            pool.wait_ge(m["info_dram"], 16 * C)
            for a in (0, C // 2):
                pool.dma_start(info[:, a:a + C // 2, :],
                               info_d[a * PN:(a + C // 2) * PN, :].rearrange("(g p) w -> p g w", p=PN)).then_inc(m["info_in"], 16)

            pool.iota(winint, [[1, NW]], base=0, channel_multiplier=0).then_inc(m["win_iota"], 1)
            pool.wait_ge(m["win_ready"], 1)
            pairs = pool.value_load(npair[0:1, 0:1], min_val=1, max_val=NW // 2 - 2)
            pool.wait_ge(m["tbl_out0"], 2 * 16 * (C // 2))
            pool.wait_ge(m["tbl_out1"], 2 * 16 * (C // 2))
            pool.wait_ge(m["pair_out"], 16)
            pool.wait_ge(m["pad_out"], 16 * 4)
            cum = [pool.alloc_register("cumP0"), pool.alloc_register("cumP1")]
            for r in cum:
                pool.reg_mov(r, 0)

            def pair_block(w, q):
                pool.wait_ge(m["bst_ready"], w + 1)
                pool.sem_inc(m["passed"], 1)
                pool.indirect_dma_start(out=blkidx[:, q, :], out_offset=None, in_=pairp_d.rearrange("(e a) -> e a", a=1),
                                        in_offset=bass.IndirectOffsetOnAxis(ap=bst[:, q:q + 1].bitcast(U32), axis=0)).then_inc(m["blk_in"], 16)

            def gather(rows, idx, q, b, done):
                for s in range(b * BLK, (b + 1) * BLK):
                    pool.indirect_dma_start(out=gath[:, q, s, :], out_offset=None, in_=rows,
                                            in_offset=bass.IndirectOffsetOnAxis(ap=idx[:, q, s:s + 1].bitcast(U32), axis=0)).then_inc(done[q], 16)

            pair_block(0, 0)
            with pool.Fori(0, pairs) as i:
                for q in range(2):
                    k = 2 * i + q
                    _, nb = window(pool, k)
                    pool.wait_ge(m["blk_in"], 16 * k + 16)
                    pool.wait_ge(m["l0_math"], k + 1)
                    pool.sem_inc(m["passed"], 1)
                    for b in range(MINB):
                        gather(table_d, blkidx, q, b, tgath)
                    if q:
                        pool.wait_ge(tgath[0], pool.snap(cum[0]) * 96)
                        pool.sem_inc(m["passed"], 1)
                    else:
                        with pool.If(i > 0):
                            pool.wait_ge(tgath[1], pool.snap(cum[1]) * 96)
                            pool.sem_inc(m["passed"], 1)
                    pair_block(k + 1, 1 - q)
                    for b in range(MINB, NBW):
                        with pool.If(nb > b):
                            gather(table_d, blkidx, q, b, tgath)
                    pool.reg_add(cum[q], cum[q], nb)
            pool.wait_ge(m["blk_in"], pairs * 32 + 16)
            pool.sem_inc(m["passed"], 1)
            pool.wait_ge(m["h2_ready"], 1)
            for c in range(C):
                pool.indirect_dma_start(out=h2_d, out_offset=bass.IndirectOffsetOnAxis(ap=nidx[:, c:c + 1].bitcast(U32), axis=0),
                                        in_=h2[:, c, :], in_offset=None).then_inc(m["h2_out"], 16)
            pool.wait_ge(m["srcp_out"], 16)
            pool.wait_ge(m["efp_out"], 16)

            def edge_block(w, q):
                pool.wait_ge(m["bst1_ready"], w + 1)
                pool.sem_inc(m["passed"], 1)
                off = bass.IndirectOffsetOnAxis(ap=bst[:, q:q + 1].bitcast(U32), axis=0)
                pool.indirect_dma_start(out=blkidx[:, q, :], out_offset=None, in_=srcp_d.rearrange("(e a) -> e a", a=1),
                                        in_offset=off).then_inc(m["src_in"], 16)
                pool.indirect_dma_start(out=efraw[:, q, :], out_offset=None, in_=efp_d.rearrange("(e d) -> e d", d=D),
                                        in_offset=off).then_inc(m["ef_in"], 16)

            sent = pool.alloc_register("sent")
            pool.reg_mov(sent, 0)

            def scatter(q):
                w = pool.snap(sent)
                pool.wait_ge(m["fin"], w + 1)
                pool.sem_inc(m["passed"], 1)
                with pool.If(w > 0):
                    pool.wait_ge(m["out_done"], w * 16)
                    pool.sem_inc(m["passed"], 1)
                pool.indirect_dma_start(out=out, out_offset=bass.IndirectOffsetOnAxis(ap=oidx[:, q:q + 1].bitcast(U32), axis=0),
                                        in_=orow[:, q, :], in_offset=None, bounds_check=N - 1, oob_is_err=False).then_inc(m["out_done"], 16)
                pool.reg_add(sent, sent, 1)

            edge_block(0, 0)
            pool.wait_ge(m["h2_out"], 16 * C)
            with pool.Fori(0, pairs) as i:
                for q in range(2):
                    k = 2 * i + q
                    _, nb = window(pool, k)
                    pool.wait_ge(m["idx_ready"], k + 1)
                    pool.wait_ge(m["h_free"], k + 1)
                    pool.sem_inc(m["passed"], 1)
                    for b in range(MINB):
                        gather(h2_d, hidx, q, b, hgath)
                    edge_block(k + 1, 1 - q)
                    for b in range(MINB, NBW):
                        with pool.If(nb > b):
                            gather(h2_d, hidx, q, b, hgath)
                    with pool.If(i > 0):
                        scatter(q)
            for q in range(2):
                scatter(q)
            pool.wait_ge(m["out_done"], pairs * 32)

        @block.tensor
        def _(pe):
            pe.wait_ge(m["const"], 2)
            pe.wait_ge(m["htan_ready"], 1)
            for t in range(C // 2):
                if t >= 12 and t % 4 == 0:
                    pe.wait_ge(m["hT_sb"], t // 4 - 2)
                last = nc.tensor.transpose(psT[0:64, t % 12, 0:PN], htan32[:, 2 * t:2 * t + 2, :].rearrange("p c k -> p (c k)"),
                                           ident[0:PN, 0:PN])
                if t % 4 == 3 or t == C // 2 - 1:
                    last.then_inc(m["hT_ps"], 1)
            pe.wait_ge(m["relw_in"], 16 * 6)
            with pe.Fori(0, C // 2) as t:
                pe.wait_ge(m["hst_sb"], t + 1)
                for j in range(2):
                    for h in range(4):
                        u = 4 * j + h
                        pe.wait_ge(m["tbl_sb"], t * 8 + (u + 1))
                        for a in range(2):
                            c0 = (2 * h + a) * PIECE
                            n = PIECE + (D if h == 3 and a else 0)
                            last = nc.tensor.matmul(psW[0:PN, u % 2, 512 * a:512 * a + n],
                                                    hst[32 * j:32 * j + D + 1, :],
                                                    relW[32 * j:32 * j + D + 1, c0:c0 + n], start=True, stop=True)
                        last.then_inc(m["tbl_ps"], 1)
            pe.wait_ge(m["info_in"], 32)
            pe.wait_ge(m["hT_sb"], (C // 2 + 3) // 4)
            nc.tensor.transpose(psT[0:C, 0, 0:PN], info[:, 0:C, 2 * D + 1], ident[0:PN, 0:PN]).then_inc(m["deg_T"], 1)
            pe.wait_ge(m["plan_col"], 1)
            nc.tensor.matmul(psT[0:C, 4, 0:1], tri[:], col[:, 2:3], start=True, stop=True)
            nc.tensor.matmul(psT[0:PN, 8, 0:1], ones[:], col[:, 2:3], start=True, stop=True).then_inc(m["plan_ps"], 1)
            pe.wait_ge(m["plan_col"], 2)
            for t in range(NW // 512):
                pe.wait_ge(m["win_psfree"], t + 1)
                for j, rhs in ((0, winhot), (1, winhot), (2, winrel)):
                    last = nc.tensor.matmul(psT[0:PN, 4 * j:4 * j + 4, :].rearrange("p a n -> p (a n)"), lhs[:, j, :],
                                            rhs[:, 512 * t:512 * t + 512], start=True, stop=True)
                last.then_inc(m["win_ps"], 1)

            pe.wait_ge(m["win_ready"], 1)
            pairs = pe.value_load(npair[0:1, 0:1], min_val=1, max_val=NW // 2 - 2)
            pe.wait_ge(m["wts_in"], 16 * 5 * BLK)
            cumt, cumb = pe.alloc_register("cumT"), pe.alloc_register("cumBp")
            pe.reg_mov(cumt, 0)
            pe.reg_mov(cumb, 0)

            def transposes(w, q):
                _, nb = window(pe, w)
                pe.wait_ge(m["idx_ready"], w + 1)
                pe.wait_ge(m["efT_sb"], pe.snap(cumt) + 1)
                for b in range(NBW):
                    with pe.If(nb > b):
                        nc.tensor.transpose(psT[0:BLK * KE, b, 0:PN],
                                            ef18[:, q, b * BLK:(b + 1) * BLK, :].rearrange("p s k -> p (s k)"),
                                            ident[0:PN, 0:PN]).then_inc(m["efT_ps"], 1)
                pe.reg_add(cumt, cumt, nb)

            def weights(w, q, b, at0):
                for s in range(2):
                    pe.wait_ge(m["w_free"], at0 + (s + 1))
                    nc.tensor.matmul(psW[0:PN, s, 0:512], efT[:, q, b, 0:PN],
                                     w[:, 3 * s:3 * s + 2, :].rearrange("k s c -> k (s c)"), start=True, stop=True)
                    nc.tensor.matmul(psW[0:PN, s, 512:768], efT[:, q, b, 0:PN],
                                     w[:, 3 * s + 2, :], start=True, stop=True).then_inc(m["w_ready"], 1)

            transposes(0, 0)
            with pe.Fori(0, pairs) as i:
                for q in range(2):
                    k = 2 * i + q
                    _, nb = window(pe, k)
                    tb = pe.snap(cumb)
                    pe.wait_ge(m["efT_sb"], tb + nb + 1)
                    for b in range(NBW):
                        with pe.If(nb > b):
                            weights(wA, q, b, tb * 4 + 2 * b)
                    transposes(k + 1, 1 - q)
                    pe.wait_ge(m["sum_read"], k + 1)
                    nc.tensor.matmul(psS[0:PN, :], zero[:, 0:PN], zero[:], start=True, stop=False)
                    weights(wM, q, 0, tb * 4 + nb * 2)
                    for b in range(NBW):
                        if b + 1 < NBW:
                            with pe.If(nb > b + 1):
                                weights(wM, q, b + 1, tb * 4 + nb * 2 + (2 * b + 2))
                        with pe.If(nb > b):
                            pe.wait_ge(m["exp_done"], tb + (b + 1))
                            for s in range(BLK):
                                nc.tensor.matmul(psS[0:PN, 0:IO], ident[0:PN, 0:PN], score[:, q, b * BLK + s, :],
                                                 start=False, stop=False)
                            pe.wait_ge(m["q_ready"], tb + (b + 1))
                            for s in range(BLK):
                                c0 = (b % 2) * BLK * IO + s * IO
                                last = nc.tensor.matmul(psS[0:PN, IO:2 * IO], ident[0:PN, 0:PN], prod[:, c0:c0 + IO],
                                                        start=False, stop=False)
                            last.then_inc(m["q_free"], 1)
                    nc.tensor.matmul(psS[0:PN, :], zero[:, 0:PN], zero[:], start=False, stop=True).then_inc(m["sum_done"], 1)
                    pe.reg_add(cumb, cumb, nb)

        @block.scalar
        def _(act):
            act.wait_ge(m["var_ready"], 1)
            nc.scalar.activation(nrm[:, 1, :], nrm[:, 0, :], ACT.Sqrt).then_inc(m["std_ready"], 1)
            act.wait_ge(m["var_ready"], 2)
            nc.scalar.activation(nrm[:, 1, :], nrm[:, 0, :], ACT.Sqrt).then_inc(m["std_ready"], 1)
            for t in range(0, C // 2, 4):
                n = min(4, C // 2 - t)
                act.wait_ge(m["hT_ps"], t // 4 + 1)
                nc.scalar.copy(hT[:, t:t + n, 0:PN], psT[0:64, t % 12:t % 12 + n, 0:PN]).then_inc(m["hT_sb"], 1)
            act.wait_ge(m["hT_sb"], (C // 2 + 3) // 4)
            with act.Fori(0, C // 2) as t:
                nc.scalar.copy(hst[:], hT[:, ds(t, 1), 0:PN].rearrange("k a n -> k (a n)")).then_inc(m["hst_sb"], 1)
                for j in range(2):
                    with act.If(t > 0):
                        act.wait_ge(m[f"tbl_out{j}"], t * 32)
                        act.sem_inc(m["passed"], 1)
                    for h in range(4):
                        u = 4 * j + h
                        act.wait_ge(m["tbl_ps"], t * 8 + (u + 1))
                        if h == 3:
                            nc.scalar.copy(rec[:, ds(2 * t + j, 1), D:2 * D].rearrange("p a d -> p (a d)"),
                                           psW[0:PN, u % 2, 512 + PIECE:512 + PIECE + D]).then_inc(m["loop_ready"], 1)
                        nc.scalar.copy(tbl[:, j, 2 * h * PIECE:(2 * h + 2) * PIECE].rearrange("p (a n) -> p a n", a=2),
                                       psW[0:PN, u % 2, :].rearrange("p (a n) -> p a n", a=2)[:, :, 0:PIECE]).then_inc(m["tbl_sb"], 1)
            act.wait_ge(m["loop_n"], 1)
            nc.scalar.activation(nrm[:, 3, :], nrm[:, 2, :], ACT.Sqrt).then_inc(m["loop_t"], 1)
            act.wait_ge(m["loop_t"], 1)
            nc.scalar.activation(nrm[:, 4, :], nrm[:, 3, :], ACT.Tanh, scale=SQC).then_inc(m["loop_t"], 1)

            act.wait_ge(m["win_ready"], 1)
            pairs = act.value_load(npair[0:1, 0:1], min_val=1, max_val=NW // 2 - 2)
            with act.Fori(0, pairs) as i:
                for q in range(2):
                    k = 2 * i + q
                    act.wait_ge(m["n2_ready"], k + 1)
                    nc.scalar.activation(sl[:, 2, :], sl[:, 1, :], ACT.Sqrt)
                    nc.scalar.drain()
                    nc.scalar.activation(sl[:, 3, :], sl[:, 2, :], ACT.Tanh, scale=SQC).then_inc(m["th_ready"], 1)
            act.wait_ge(m["hnorm"], 1)
            nc.scalar.activation(nrm[:, 1, :], nrm[:, 0, :], ACT.Sqrt).then_inc(m["hnorm_out"], 1)
            act.wait_ge(m["hnorm"], 2)
            nc.scalar.activation(nrm[:, 1, :], nrm[:, 0, :], ACT.Sqrt).then_inc(m["hnorm_out"], 1)
            act.wait_ge(m["hnorm"], 3)
            nc.scalar.activation(nrm[:, 1, :], nrm[:, 0, :], ACT.Sqrt).then_inc(m["hnorm_out"], 1)

            cumt, cumb = act.alloc_register("cumTa"), act.alloc_register("cumBa")
            act.reg_mov(cumt, 0)
            act.reg_mov(cumb, 0)

            def copies(w, q):
                _, nb = window(act, w)
                tt = act.snap(cumt)
                act.wait_ge(m["efT_ps"], tt + nb)
                act.sem_inc(m["passed"], 1)
                with act.Fori(0, nb) as b:
                    nc.scalar.copy(efT[:, q, ds(b, 1), 0:PN].rearrange("k a n -> k (a n)"),
                                   psT[0:BLK * KE, ds(b, 1), 0:PN].rearrange("k a n -> k (a n)")).then_inc(m["efT_sb"], 1)
                act.reg_add(cumt, cumt, nb)

            copies(0, 0)
            with act.Fori(0, pairs) as i:
                for q in range(2):
                    k = 2 * i + q
                    copies(k + 1, 1 - q)
                    _, nb = window(act, k)
                    tb = act.snap(cumb)
                    act.wait_ge(m["d_ready"], k + 1)
                    nc.scalar.activation(cfac, diff, ACT.Exp).then_inc(m["c_ready"], 1)
                    with act.Fori(0, nb) as b:
                        act.wait_ge(m["sub_done"], tb + b + 1)
                        v = score[:, q, ds(b * BLK, BLK), :]
                        nc.scalar.activation(v, v, ACT.Exp).then_inc(m["exp_done"], 1)
                    act.reg_add(cumb, cumb, nb)

        @block.vector
        def _(dve):
            V = nc.vector
            for name, n in (("tbl_sb", 2), ("l0_math", 2), ("h_free", 2), ("efT_sb", 1), ("w_free", 2), ("q_free", 2),
                            ("sum_read", 1), ("win_psfree", 1)):
                dve.sem_inc(m[name], n)
            V.memset(stage[:], 0.0)
            V.memset(wA[:], 0.0)
            V.memset(wM[:], 0.0)
            V.memset(negbig[:], -BIG)
            V.memset(pad1[:], 1.0)
            V.memset(gath[:], 0.0)
            V.memset(zero[:], 0.0)
            V.memset(ones[:], 1.0)
            V.memset(info[:], 0.0)
            V.memset(npad[:], float(N))
            V.memset(lamsum[:], 0.0)
            V.memset(work[:], 0.0)
            V.memset(xnew[:], 0.0)
            V.drain().then_inc(m["wzero"], 1)

            def row_sum(o, i):
                V.tensor_reduce(o, i, AX.X, ALU.add)
                V.drain()

            def tt(o, a, b, op):
                V.tensor_tensor(o, a, b, op)
                V.drain()

            def ts(o, a, s1, s2, op0, op1=None):
                if op1 is None:
                    V.tensor_scalar(o, a, s1, None, op0)
                else:
                    V.tensor_scalar(o, a, s1, s2, op0, op1)
                V.drain()

            def norm_relu(o, i, t0, to_act, from_act, n):
                row_sum(nrm[:, 2, :], i)
                ts(nrm[:, 2, :], nrm[:, 2, :], 1.0 / D, None, ALU.mult)
                tt(t0, i, bc(nrm[:, 2, :], D), ALU.subtract)
                tt(o, t0, t0, ALU.mult)
                row_sum(nrm[:, 2, :], o)
                V.tensor_scalar(nrm[:, 0, :], nrm[:, 2, :], 1.0 / D, LN_EPS, ALU.mult, ALU.add).then_inc(to_act, 1)
                dve.wait_ge(from_act, n)
                V.reciprocal(nrm[:, 2, :], nrm[:, 1, :])
                V.drain()
                tt(t0, t0, bc(nrm[:, 2, :], D), ALU.mult)
                ts(o, t0, 0.0, None, ALU.max)

            dve.wait_ge(m["x_in"], 16)
            h, t0, t1 = tmp(0), tmp(1), tmp(2)
            norm_relu(h, rec[:, :, 0:D], t0, m["var_ready"], m["std_ready"], 1)
            tt(t0, h, h, ALU.mult)
            row_sum(nrm[:, 2, :], t0)
            V.tensor_scalar(nrm[:, 0, :], nrm[:, 2, :], MIN_NORM, None, ALU.max).then_inc(m["var_ready"], 1)
            dve.wait_ge(m["std_ready"], 2)
            z, z2, acc = nrm[:, 2, :], nrm[:, 3, :], nrm[:, 4, :]
            ts(z, nrm[:, 1, :], SQC, 1.0 - BALL, ALU.mult, ALU.min)
            tt(z2, z, z, ALU.mult)
            ts(acc, z2, 1.0 / 23, 1.0 / 21, ALU.mult, ALU.add)
            for n in range(19, 0, -2):
                tt(acc, acc, z2, ALU.mult)
                ts(acc, acc, 1.0 / n, None, ALU.add)
            tt(t0, h, bc(acc, D), ALU.mult)
            V.memset(htan32[:, :, D:D + 1], 1.0)
            V.tensor_copy(htan32[:, :, 0:D], t0)
            V.drain().then_inc(m["htan_ready"], 1)

            dve.wait_ge(m["dst_in"], 16)
            V.tensor_copy(firsts[:], dst_sb.rearrange("p (r w) -> p r w", w=ROW)[:, :, 0]).then_inc(m["firsts_ready"], 1)
            dve.wait_ge(m["const"], 2)
            V.tensor_copy(nodeid[:], nodei[:])
            V.tensor_copy(iotaf[:], iotai[:])
            V.drain()
            dve.wait_ge(m["firstrow_in"], 16)
            for c in range(C + 1):
                V.tensor_scalar(junk[:, 0:NROW], firstrow, nodeid[:, c:c + 1], 0.0, ALU.is_lt, ALU.add,
                                accum_out=cnt[:, c:c + 1])
                V.drain()
            ts(cnt[:], cnt[:], -1.0, 0.0, ALU.add, ALU.max)
            V.tensor_copy(rowi[:], cnt[:]).then_inc(m["rows_ready"], 1)
            dve.wait_ge(m["edges_in"], 32)
            V.scalar_tensor_tensor(pair_sb, src_sb, float(R), et_sb, ALU.mult, ALU.add).then_inc(m["pair_ready"], 1)
            dve.wait_ge(m["rows_in"], 16 * (C + 1))
            tt(less, dstblk, bc(nodeid[:], ROW), ALU.is_lt)
            row_sum(start0[:], less)
            V.scalar_tensor_tensor(start0[:], cnt[:], float(ROW), start0[:], ALU.mult, ALU.add)
            V.drain()
            tt(rec[:, :, 2 * D + 1], start0[:, 1:C + 1], start0[:, 0:C], ALU.subtract)
            V.tensor_copy(rec[:, :, 2 * D], start0[:, 0:C])
            V.tensor_copy(rec[:, :, 2 * D + 2], nodeid[:, 0:C])
            V.memset(rec[:, :, 2 * D + 3:2 * D + 4], 0.0)
            ts(key[:], rec[:, :, 2 * D + 1], 1023.0, 8192.0, ALU.min, ALU.mult)
            V.scalar_tensor_tensor(key[:], nodeid[:, 0:C], -1.0, key[:], ALU.mult, ALU.add).then_inc(m["key_ready"], 1)
            dve.wait_ge(m["keyrow_in"], 16)
            for c in range(C):
                V.tensor_scalar(junk, keyrow, key[:, c:c + 1], 0.0, ALU.is_gt, ALU.add, accum_out=rank[:, c:c + 1])
                V.drain()
            V.tensor_copy(ranki[:], rank[:])
            dve.wait_ge(m["loop_ready"], C)
            lp = rec[:, :, D:2 * D]
            tt(t0, lp, lp, ALU.mult)
            row_sum(nrm[:, 2, :], t0)
            V.tensor_scalar(nrm[:, 2, :], nrm[:, 2, :], MIN_NORM, None, ALU.max)
            V.drain().then_inc(m["loop_n"], 1)
            dve.wait_ge(m["loop_t"], 2)
            ts(nrm[:, 3, :], nrm[:, 3, :], SQC, None, ALU.mult)
            V.reciprocal(nrm[:, 5, :], nrm[:, 3, :])
            V.drain()
            tt(nrm[:, 4, :], nrm[:, 4, :], nrm[:, 5, :], ALU.mult)
            tt(lp, lp, bc(nrm[:, 4, :], D), ALU.mult)
            V.drain().then_inc(m["rec_ready"], 1)

            dve.wait_ge(m["deg_T"], 1)
            V.tensor_reduce(col[:, 0:1], psT[0:C, 0, 0:PN], AX.X, ALU.max)
            V.drain()
            MAGIC = 8388608.0

            def ceil_div(o, i, n):
                ts(o, i, 1.0, None, ALU.max)
                ts(o, o, (n - 1) / 2.0, 1.0 / n, ALU.add, ALU.mult)
                ts(o, o, MAGIC, None, ALU.add)
                ts(o, o, -MAGIC, None, ALU.add)

            ceil_div(col[:, 1:2], col[:, 0:1], BLK)
            ceil_div(col[:, 2:3], col[:, 1:2], NBW)
            V.drain().then_inc(m["plan_col"], 1)
            dve.wait_ge(m["plan_ps"], 1)
            V.tensor_copy(col[:, 3:4], psT[0:C, 4, 0:1])
            V.tensor_copy(npairf[:], psT[0:PN, 8, 0:1])
            V.drain()
            tt(col[:, 4:5], col[:, 3:4], col[:, 2:3], ALU.subtract)
            ts(npairf[:], npairf[:], 0.5, 0.25, ALU.mult, ALU.add)
            ts(npairf[:], npairf[:], MAGIC, None, ALU.add)
            ts(npairf[:], npairf[:], -MAGIC, None, ALU.add)
            V.tensor_copy(npair[:], npairf[:])
            dve.wait_ge(m["win_iota"], 1)
            V.tensor_copy(winpos, winint)
            V.drain()
            V.tensor_scalar(winrel, winpos, col[:, 3:4], None, ALU.is_ge)
            V.drain()
            V.scalar_tensor_tensor(winhot, winpos, col[:, 4:5], winrel, ALU.is_ge, ALU.subtract)
            V.drain()
            V.scalar_tensor_tensor(winrel, winpos, col[:, 4:5], winhot, ALU.subtract, ALU.mult)
            ts(col[:, 5:6], nodeid[0:C, 0:1], 1.0 / C, None, ALU.mult)
            ts(col[:, 5:6], col[:, 5:6], MAGIC, None, ALU.add)
            ts(col[:, 5:6], col[:, 5:6], -MAGIC, None, ALU.add)
            ts(col[:, 5:6], col[:, 5:6], -float(C), None, ALU.add)
            for j, cc in ((0, 5), (1, 1)):
                ts(lhs[:, j, :], ones[:], col[:, cc:cc + 1], None, ALU.mult)
            V.tensor_copy(lhs[:, 2, :], ones[:])
            V.drain().then_inc(m["plan_col"], 1)
            wv = wvt
            for t in range(NW // 512):
                dve.wait_ge(m["win_ps"], t + 1)
                pg, pn, pr = (psT[0:PN, 4 * j:4 * j + 4, :].rearrange("p a n -> p (a n)") for j in range(3))
                V.tensor_copy(tabs[:, 512 * t:512 * t + 512], pr)
                V.tensor_copy(wv[:, 0, :], pr)
                V.drain()
                V.scalar_tensor_tensor(wv[:, 0, :], wv[:, 0, :], -float(NBW), pn, ALU.mult, ALU.add)
                V.tensor_scalar(wv[:, 1, :], pg, float(NBW), float(NBW * C - 1), ALU.mult, ALU.add)
                V.drain().then_inc(m["win_psfree"], 1)
                ts(wv[:, 0, :], wv[:, 0, :], float(NBW), float(MINB), ALU.min, ALU.max)
                tt(tabgn[:, 512 * t:512 * t + 512], wv[:, 1, :], wv[:, 0, :], ALU.add)
            V.tensor_copy(nidx[:, 0:C], info[:, 0:C, 2 * D + 2])
            V.tensor_copy(nidx[:, C:C + 1], npad[:])
            V.memset(numer, 0.0)
            V.drain().then_inc(m["win_ready"], 1)
            pairs = dve.value_load(npair[0:1, 0:1], min_val=1, max_val=NW // 2 - 2)

            start = info[:, :, 2 * D]
            deg = info[:, :, 2 * D + 1]

            def window_start(w, q, done):
                g, _ = window(dve, w)
                n = tabs[:, ds(w, 1)]
                V.scalar_tensor_tensor(bstf[:, q:q + 1], n, float(S), start[:, ds(g, 1)], ALU.mult, ALU.add)
                V.scalar_tensor_tensor(rem[:, q:q + 1], n, -float(S), deg[:, ds(g, 1)], ALU.mult, ALU.add)
                V.tensor_scalar(keep[:, q:q + 1], n, 1.0, None, ALU.min)
                V.drain()
                V.tensor_scalar(keepbig[:, q:q + 1], keep[:, q:q + 1], -1.0, BIG, ALU.add, ALU.mult)
                V.tensor_scalar(bst[:, q:q + 1], bstf[:, q:q + 1], float(E), None, ALU.min)
                V.drain().then_inc(done, 1)

            cum = [dve.alloc_register("cumV0"), dve.alloc_register("cumV1")]
            for r in cum:
                dve.reg_mov(r, 0)
            window_start(0, 0, m["bst_ready"])
            with dve.Fori(0, pairs) as i:
                for q in range(2):
                    k = 2 * i + q
                    G = gath[:, q, :, :]
                    g, nb = window(dve, k)
                    dve.reg_add(cum[q], cum[q], nb)
                    V.tensor_scalar(valid[:, q, :], iotaf[:], rem[:, q:q + 1], None, ALU.is_lt)
                    if q:
                        dve.wait_ge(m["blk_in"], 16 * k)
                        dve.sem_inc(m["passed"], 1)
                    else:
                        with dve.If(i > 0):
                            dve.wait_ge(m["blk_in"], 16 * k)
                            dve.sem_inc(m["passed"], 1)
                    window_start(k + 1, 1 - q, m["bst_ready"])
                    dve.wait_ge(tgath[q], dve.snap(cum[q]) * 96)
                    tt(sq, G, G, ALU.mult)
                    row_sum(sl[:, 0, :], sq)
                    V.tensor_scalar(sl[:, 1, :], sl[:, 0, :], MIN_NORM, None, ALU.max).then_inc(m["n2_ready"], 1)
                    dve.wait_ge(m["th_ready"], k + 1)
                    ts(sl[:, 2, :], sl[:, 2, :], SQC, None, ALU.mult)
                    V.reciprocal(sl[:, 4, :], sl[:, 2, :])
                    V.drain()
                    tt(sl[:, 3, :], sl[:, 3, :], sl[:, 4, :], ALU.mult)
                    tt(sl[:, 4, :], sl[:, 3, :], sl[:, 3, :], ALU.mult)
                    tt(sl[:, 4, :], sl[:, 4, :], sl[:, 0, :], ALU.mult)
                    ts(sl[:, 4, :], sl[:, 4, :], -CURV, 1.0, ALU.mult, ALU.add)
                    ts(sl[:, 4, :], sl[:, 4, :], EPS, 0.5, ALU.add, ALU.mult)
                    V.reciprocal(sl[:, 5, :], sl[:, 4, :])
                    V.drain()
                    tt(sl[:, 5, :], sl[:, 5, :], valid[:, q, :], ALU.mult)
                    row_sum(lsum[:], sl[:, 5, :])
                    tt(sl[:, 3, :], sl[:, 3, :], sl[:, 5, :], ALU.mult)
                    V.tensor_tensor(sq, G, bc(sl[:, 3, :], D), ALU.mult)
                    V.drain().then_inc(m["l0_math"], 1)
                    row_sum(nsum[:], sq.rearrange("p s d -> p d s"))
                    V.tensor_tensor(numer[:, ds(g, 1), :].rearrange("p a d -> p (a d)"),
                                    numer[:, ds(g, 1), :].rearrange("p a d -> p (a d)"), nsum[:], ALU.add)
                    V.tensor_tensor(lamsum[:, ds(g, 1)], lamsum[:, ds(g, 1)], lsum[:], ALU.add)
                    V.drain()

            A, B, T = tmp(0), tmp(1), tmp(2)
            X0, Y = info[:, 0:C, 0:D], info[:, 0:C, D:2 * D]
            n0, n1, n2, n3, n4, n5 = (nrm[:, j, :] for j in (2, 3, 4, 5, 6, 7))
            V.tensor_scalar(nrm[:, 0, :], deg[:, 0:C], 1.0, None, ALU.max).then_inc(m["hnorm"], 1)
            dve.wait_ge(m["hnorm_out"], 1)
            V.reciprocal(n0, nrm[:, 1, :])
            V.drain()
            tt(n1, n0, deg[:, 0:C], ALU.mult)
            ts(n1, n1, EPS, None, ALU.add)
            V.reciprocal(n2, n1)
            V.drain()
            tt(n0, n0, n2, ALU.mult)
            tt(n1, n0, lamsum[:, 0:C], ALU.mult)
            ts(n1, n1, EPS, None, ALU.add)
            V.reciprocal(n2, n1)
            V.drain()
            tt(n0, n0, n2, ALU.mult)
            tt(A, numer[:, 0:C, :], bc(n0, D), ALU.mult)
            tt(T, A, A, ALU.mult)
            row_sum(n0, T)
            V.tensor_scalar(nrm[:, 0, :], n0, MIN_NORM, None, ALU.max).then_inc(m["hnorm"], 1)
            dve.wait_ge(m["hnorm_out"], 2)
            V.reciprocal(n1, nrm[:, 1, :])
            V.drain()
            ts(n1, n1, (1.0 - BALL) / SQC, 1.0, ALU.mult, ALU.min)
            tt(A, A, bc(n1, D), ALU.mult)
            tt(T, A, A, ALU.mult)
            row_sum(n0, T)
            tt(T, Y, Y, ALU.mult)
            row_sum(n1, T)
            tt(T, A, Y, ALU.mult)
            row_sum(n2, T)
            ts(n3, n2, 2.0 * CURV, 1.0, ALU.mult, ALU.add)
            tt(n4, n0, n1, ALU.mult)
            V.scalar_tensor_tensor(n4, n4, CURV * CURV, n3, ALU.mult, ALU.add)
            V.scalar_tensor_tensor(n3, n1, CURV, n3, ALU.mult, ALU.add)
            V.drain()
            ts(n4, n4, MIN_NORM, None, ALU.max)
            V.reciprocal(n5, n4)
            ts(n0, n0, -CURV, 1.0, ALU.mult, ALU.add)
            tt(T, A, bc(n3, D), ALU.mult)
            tt(B, Y, bc(n0, D), ALU.mult)
            tt(T, T, B, ALU.add)
            tt(T, T, bc(n5, D), ALU.mult)
            tt(xnew[:, 0:C, :], X0, T, ALU.add)
            norm_relu(h2[:], xnew[:, 0:C, :], tmp(3), m["hnorm"], m["hnorm_out"], 3)
            V.drain().then_inc(m["h2_ready"], 1)

            V.memset(mnew, 0.0)
            V.memset(total, 0.0)
            V.drain()
            sent = dve.alloc_register("sentV")
            dve.reg_mov(sent, 0)
            cumb = dve.alloc_register("cumBv")
            dve.reg_mov(cumb, 0)
            for r in cum:
                dve.reg_mov(r, 0)

            def edge_prep(w, q):
                dve.wait_ge(m["src_in"], 16 * w + 16)
                dve.wait_ge(m["ef_in"], 16 * w + 16)
                ts(valid[:, q, :], iotaf[:], rem[:, q:q + 1], None, ALU.is_lt)
                V.scalar_tensor_tensor(valid2[:], blkidx[:, q, :], -float(N), valid[:, q, :], ALU.add, ALU.mult)
                V.tensor_tensor(ef18[:, q, :, 0:D], efraw[:, q, 0:S * D].rearrange("p (s d) -> p s d", d=D),
                                bc(valid[:, q, :], D), ALU.mult)
                V.tensor_copy(ef18[:, q, :, D], valid[:, q, :])
                V.tensor_scalar(ef18[:, q, :, D + 1], valid[:, q, :], -1.0, 1.0, ALU.mult, ALU.add)
                V.drain()
                V.tensor_scalar(hidx[:, q, :], valid2[:], float(N), None, ALU.add)
                V.drain().then_inc(m["idx_ready"], 1)

            dve.wait_ge(m["blk_in"], pairs * 32 + 16)
            dve.sem_inc(m["passed"], 1)
            window_start(0, 0, m["bst1_ready"])
            window_start(1, 1, m["bst1_ready"])
            edge_prep(0, 0)
            with dve.Fori(0, pairs) as i:
                for q in range(2):
                    k = 2 * i + q
                    edge_prep(k + 1, 1 - q)
                    g, nb = window(dve, k)
                    tb = dve.snap(cumb)
                    dve.reg_add(cum[q], cum[q], nb)
                    V.tensor_scalar(mold, mnew[:, 1 - q, :], keep[:, q:q + 1], keepbig[:, q:q + 1], ALU.mult, ALU.add)
                    V.tensor_scalar(total, total, keep[:, q:q + 1], None, ALU.mult)
                    V.drain()
                    window_start(k + 2, q, m["bst1_ready"])
                    dve.wait_ge(hgath[q], dve.snap(cum[q]) * 96)

                    def times_h(dst_ap, b, s, at0):
                        dve.wait_ge(m["w_ready"], at0 + (s + 1))
                        hb = gath[:, q, ds(b * BLK + 3 * s, 3), :]
                        V.tensor_tensor(dst_ap.rearrange("p s (i o) -> p s i o", o=D),
                                        psW[0:PN, s, 0:3 * IO].rearrange("p (s i o) -> p s i o", i=D, o=D),
                                        bc(hb, D), ALU.mult).then_inc(m["w_free"], 1)

                    def scores(b):
                        for s in range(2):
                            times_h(score[:, q, ds(b * BLK + 3 * s, 3), :], b, s, tb * 4 + b * 2)
                        V.drain()

                    scores(0)
                    scores(1)
                    V.tensor_tensor(macc, score[:, q, 0:BLK, :], score[:, q, BLK:2 * BLK, :], ALU.max)
                    with dve.Fori(2, nb) as b:
                        scores(b)
                        V.tensor_tensor(macc, macc, score[:, q, ds(b * BLK, BLK), :], ALU.max)
                    V.drain()
                    V.tensor_reduce(mred, macc.rearrange("p s c -> p c s"), AX.X, ALU.max)
                    V.drain()
                    tt(mnew[:, q, :], mred, mold, ALU.max)
                    V.tensor_tensor(diff, mold, mnew[:, q, :], ALU.subtract).then_inc(m["d_ready"], 1)

                    with dve.Fori(0, nb) as b:
                        blk = score[:, q, ds(b * BLK, BLK), :]
                        V.tensor_tensor(blk, blk, mnew[:, q, :].unsqueeze(1).to_broadcast([PN, BLK, IO]),
                                        ALU.subtract).then_inc(m["sub_done"], 1)
                        dve.wait_ge(m["q_free"], tb + b + 1)
                        par = (b % 2) * (BLK * IO)
                        for s in range(2):
                            times_h(prod[:, ds(par + 3 * s * IO, 3 * IO)].rearrange("p (s c) -> p s c", c=IO), b, s,
                                    tb * 4 + nb * 2 + b * 2)
                        V.drain()
                        dve.wait_ge(m["exp_done"], tb + b + 1)
                        pr = prod[:, ds(par, BLK * IO)]
                        V.tensor_tensor(pr, pr, blk.rearrange("p s c -> p (s c)"), ALU.mult).then_inc(m["q_ready"], 1)
                    V.drain().then_inc(m["h_free"], 1)
                    dve.reg_add(cumb, cumb, nb)
                    dve.wait_ge(m["c_ready"], k + 1)
                    tt(total, total, cfac.unsqueeze(1).to_broadcast([PN, 2, IO]), ALU.mult)
                    dve.wait_ge(m["sum_done"], k + 1)
                    V.tensor_tensor(total, total, psS[0:PN, :].rearrange("p (a c) -> p a c", a=2), ALU.add)
                    V.drain().then_inc(m["sum_read"], 1)
                    V.reciprocal(ratio, total[:, 0, :])
                    V.drain()
                    tt(ratio, ratio, total[:, 1, :], ALU.mult)
                    row_sum(ft[:], ratio.rearrange("p (i o) -> p o i", o=D))
                    with dve.If(i > 0):
                        dve.reg_add(sent, sent, 16)
                        dve.wait_ge(m["out_done"], dve.snap(sent))
                        dve.sem_inc(m["passed"], 1)
                    V.tensor_tensor(orow[:, q, :], ft[:], xnew[:, ds(g, 1), :].rearrange("p a d -> p (a d)"), ALU.add)
                    V.tensor_copy(oidx[:, q:q + 1], nidx[:, ds(g, 1)])
                    V.drain().then_inc(m["fin"], 1)


_INS = ["x", "src", "dst", "edge_attr_16", "edge_type_230", "L0_gnn_rel_weight", "L0_gnn_loop_weight", "L0_gnn_rel_emb",
        "L1_gnn_W_msg", "L1_gnn_b_msg", "L1_gnn_W_attn", "L1_gnn_b_attn"]


def kernel(**inputs):
    import numpy as _np
    import concourse.bacc as _bacc
    from concourse.bass_utils import run_bass_kernel_spmd as _run

    nc = _bacc.Bacc("TRN2", target_bir_lowering=False, num_devices=1)
    arrays, args = {}, []
    for name in _INS:
        a = _np.ascontiguousarray(inputs[name])
        arrays[f"in_{name}"] = a
        args.append(nc.dram_tensor(f"in_{name}", a.shape, mybir.dt.from_np(a.dtype), kind="ExternalInput").ap())
    out = nc.dram_tensor("out_0", (N, D), F32, kind="ExternalOutput").ap()
    scratch = [nc.dram_tensor(n, s, t, kind="Internal").ap() for n, s, t in (
        ("table", (N * R, D), F32), ("srcp", (E + S,), I32), ("pairp", (E + S,), I32), ("efp", ((E + S) * D,), F32),
        ("h2_dram", (N + 1, D), F32), ("first_dram", (NROW,), F32), ("key_dram", (N,), F32), ("info_dram", (N, INFO), F32))]
    build(nc, *args, out, scratch)
    r = _run(nc, [arrays], core_ids=[0])
    return r.results[0]["out_0"]
```

```python
from contextlib import ExitStack

import concourse.bass as bass
from concourse import mybir

F32 = mybir.dt.float32
BF16 = mybir.dt.bfloat16
I32 = mybir.dt.int32
I16 = mybir.dt.int16
U32 = mybir.dt.uint32
ALU = mybir.AluOpType
ACT = mybir.ActivationFunctionType
AX = mybir.AxisListType
ds = bass.ds

N, D, E, R = 6250, 16, 206250, 230
PN = 125
C = N // PN
IO = D * D
BLK = 6
NBW = 8
S = BLK * NBW
MINB = 3
NW = 4608
KE = 6 * D + 4
HI, MID, LO = 0, 3 * D, 5 * D
RING = 3
RO = R * D
PIECE = RO // 8
ROW = 110
NROW = E // ROW
RPP = NROW // PN
EPP = E // PN
INFO = 2 * D + 4

BIG = 2.0 ** 120
CURV = 0.01
SQC = 0.1
EPS = 1e-6
MIN_NORM = 1e-10
BALL = 1e-5
LN_EPS = 1e-5


def build(nc, x, src, dst, efeat, etype, relw, loopw, relemb, wmsg, bmsg, wattn, battn, out, scratch):
    table_d, srcp_d, pairp_d, efp_d, h2_d, first_d, key_d, info_d = scratch
    ctx = ExitStack()
    with ctx:
        def sb(name, shape, dt=F32):
            return ctx.enter_context(nc.sbuf_tensor(name, shape, dt))

        def sem(name):
            return ctx.enter_context(nc.semaphore(name))

        arena = sb("arena", [128, 2 * S * IO])

        def at(off, n, p=PN, dt=F32):
            v = arena[0:p, off:off + n]
            return v if dt is F32 else v.bitcast(dt)

        score = arena[0:PN, :].rearrange("p (q s c) -> p q s c", q=2, c=IO)
        tbl = at(0, 2 * RO).rearrange("p (q n) -> p q n", q=2)
        o = 2 * RO
        firstrow = at(o, NROW)
        dstblk = at(o + NROW, (C + 1) * ROW, dt=I32).rearrange("p (c w) -> p c w", w=ROW)
        dst_sb = at(o + NROW, EPP, dt=I32)
        keyrow = at(o, N)
        junk = at(o + NROW + (C + 1) * ROW, N)
        less = junk[:, 0:(C + 1) * ROW].rearrange("p (c w) -> p c w", w=ROW)
        winint, winpos = at(o, NW, C, I32), at(o, NW, C)
        winhot, winrel = at(o + NW, NW, C), at(o + 2 * NW, NW, C)
        rec = at(22700, C * INFO).rearrange("p (c w) -> p c w", w=INFO)

        def tmp(i):
            return at(o + NROW + (C + 1) * ROW + i * C * D, C * D).rearrange("p (c d) -> p c d", d=D)

        stage = sb("stage", [128, RING * BLK * IO + S * KE // 2 + S * 126])
        prod = stage[0:PN, 0:RING * BLK * IO]
        o2 = RING * BLK * IO
        efs = stage[0:PN, o2:o2 + S * KE // 2].bitcast(BF16).rearrange("p (s k) -> p s k", k=KE)
        o2 += S * KE // 2
        efT = stage[0:KE, o2:o2 + S * 126].bitcast(BF16).rearrange("k (q s n) -> k q s n", q=2, n=126)
        tabtmp = stage[0:1, o2:o2 + NW // 2].bitcast(I16)
        wraw, wres = stage[0:D + 1, 9500:9500 + 2 * IO], stage[0:D + 1, 10012:10012 + 2 * IO]
        wparts = stage[0:D + 1, 10524:10524 + 3 * IO].bitcast(BF16).rearrange("k (j n) -> k j n", j=3)
        relW = stage[0:64, 0:RO + D]
        htan32 = stage[0:PN, 3700:3700 + C * 32].rearrange("p (c k) -> p c k", k=32)
        numer = stage[0:PN, 0:(C + 1) * D].rearrange("p (c d) -> p c d", d=D)

        work = sb("work", [128, BLK * IO + 10 * IO])
        hT = work[0:64, 0:(C // 2) * 128].rearrange("k (m n) -> k m n", n=128)
        sq = work[0:PN, 0:S * D].rearrange("p (s d) -> p s d", d=D)
        sl = work[0:PN, S * D:S * D + 6 * S].rearrange("p (j s) -> p j s", s=S)
        macc = work[0:PN, 0:BLK * IO].rearrange("p (s c) -> p s c", c=IO)

        def col256(j, n=1):
            return work[0:PN, BLK * IO + j * IO:BLK * IO + (j + n) * IO]

        mold, ratio = col256(0), col256(1)
        mred = ratio
        total = col256(2, 2).rearrange("p (a c) -> p a c", a=2)
        mnew = col256(4, 2).rearrange("p (q c) -> p q c", q=2)
        diff = col256(6, 2).rearrange("p (q c) -> p q c", q=2)
        cfac = col256(8, 2).rearrange("p (q c) -> p q c", q=2)

        gath = sb("gath", [PN, 2, S, D])
        efraw = sb("efraw", [PN, 2, max(S * D, EPP // 2)])
        src_sb = stage[0:PN, 5300:5300 + EPP].bitcast(I32)
        et_sb = efraw[:, :, :].rearrange("p q n -> p (q n)")[:, 0:EPP].bitcast(I32)
        pair_sb = et_sb
        efin = efraw[:, 0, 0:S * D].rearrange("p (s d) -> p s d", d=D)
        efres = efraw[:, 1, 0:S * D].rearrange("p (s d) -> p s d", d=D)
        wst = sb("wst", [KE, 2 * IO], BF16)
        info = sb("info", [PN, C + 1, INFO])
        xnew = sb("xnew", [PN, C + 1, D])
        h2 = tmp(4)
        lamsum = sb("lamsum", [PN, C + 1])
        hst = sb("hst", [64, PN])
        tabs = sb("tabs", [128, NW], I16)
        tabgn = tabs[127:128, :]
        ident = sb("ident", [128, 128])
        identb = sb("identb", [128, 128], BF16)
        tri = sb("tri", [C, C])
        ones = sb("ones", [C, PN])
        zero = sb("zero", [1, 512], BF16)
        urow = sb("urow", [1, 2 * IO], BF16)
        pad1 = sb("pad1", [1, D])
        padrow = gath[0:1, 0, :, :].rearrange("p s d -> p (s d)")
        nodei = sb("nodei", [PN, C + 1], I32)
        nodeid = sb("nodeid", [PN, C + 1])
        iotai = sb("iotai", [PN, S], I32)
        iotaf = sb("iotaf", [PN, S])
        firsts = sb("firsts", [PN, RPP])
        cnt = sb("cnt", [PN, C + 1])
        rowi = sb("rowi", [PN, C + 1], I32)
        start0 = sb("start0", [PN, C + 1])
        key = sb("key", [PN, C])
        rank = sb("rank", [PN, C])
        ranki = sb("ranki", [PN, C], I32)
        nidx = sb("nidx", [PN, C + 1], I32)
        col = sb("col", [C, 8])
        lhs = sb("lhs", [C, 3, PN])
        npairf = sb("npairf", [PN, 1])
        npair = sb("npair", [PN, 1], I32)
        nrm = sb("nrm", [PN, 8, C])
        bstf = sb("bstf", [PN, 2])
        bst = sb("bst", [PN, 2], I32)
        rem = sb("rem", [PN, 2])
        keep = sb("keep", [PN, 2])
        keepbig = sb("keepbig", [PN, 2])
        blkidx = sb("blkidx", [PN, 2, S], I32)
        hidx = sb("hidx", [PN, 2, S], I32)
        valid = sb("valid", [PN, 2, S])
        wvt = work[0:PN, 0:1024].rearrange("p (a n) -> p a n", a=2)
        valid2 = sb("valid2", [PN, S])
        npad = sb("npad", [PN, 1])
        lsum = sb("lsum", [PN, 1])
        nsum = sb("nsum", [PN, D])
        gx = sb("gx", [PN, 2, D + 1])
        gid = sb("gid", [PN, 2], I32)
        orow = sb("orow", [PN, 2, D])
        oidx = sb("oidx", [PN, 2], I32)
        ft = sb("ft", [PN, D])

        psW = ctx.enter_context(nc.psum_tensor("psW", [128, 2, 1024], F32))
        psS = ctx.enter_context(nc.psum_tensor("psS", [128, 512], F32))
        psT = ctx.enter_context(nc.psum_tensor("psT", [128, 12, 128], F32))
        psTb = psT[:, :, :].rearrange("p a n -> p (a n)").bitcast(BF16).rearrange("p (t s n) -> p t s n", t=3, n=128)

        names = ("x_in dst_in edges_in relw_in wts_in wzero const node_tmp var_ready std_ready htan_ready hT_ps hT_sb "
                 "tbl_ps tbl_psfree tbl_sb tbl_out0 tbl_out1 firsts_ready firsts_dram firstrow_in rows_ready rows_in "
                 "key_ready key_dram keyrow_in pair_ready pair_out srcp_out efp_out pad_out "
                 "loop_ready hst_sb rec_ready info_dram info_in deg_T deg_red plan_col plan_ps win_ready win_ps win_psfree "
                 "passed tab_ready wraw_in wsplit win_iota loop_n loop_t loop_norm tab_done "
                 "bst_ready blk_in tg0 tg1 l0_math n2_ready th_ready hnorm hnorm_out x2_var x2_std h2_ready h2_out "
                 "bst1_ready src_in ef_in idx_ready hi_done res_done mid_done ef_ready raw_free hg0 hg1 h_free efT_ps efT_sb w_ready w_free d_ready c_ready "
                 "sub_done exp_done q_ready q_free sum_done sum_read fin out_done init credit").split()
        m = {n: sem("s_" + n) for n in names}
        tgath, hgath = (m["tg0"], m["tg1"]), (m["hg0"], m["hg1"])

        block = ctx.enter_context(nc.Block())

        def bc(v, n):
            return v.unsqueeze(len(v.shape)).to_broadcast(list(v.shape) + [n])

        def window(eng, k):
            v = eng.value_load(tabgn[:, ds(k, 1)], min_val=0, max_val=C * NBW + NBW - 1)
            return v // NBW, v % NBW + 1

        @block.sync
        def _(sp):
            sp.dma_start(rec[:, :, 0:D], x.rearrange("(p c) d -> p c d", p=PN)).then_inc(m["x_in"], 16)
            sp.dma_start(dst_sb, dst.rearrange("(p e) -> p e", p=PN)).then_inc(m["dst_in"], 16)
            sp.wait_ge(m["wzero"], 1)
            for j in range(2):
                p = 32 * j
                sp.dma_start(relW[p:p + D, 0:RO].rearrange("i (r o) -> i r o", o=D),
                             relw.rearrange("r i o -> i r o")).then_inc(m["relw_in"], 16)
                sp.dma_start(relW[p + D:p + D + 1, 0:RO], relemb.rearrange("(a r) o -> a (r o)", a=1)).then_inc(m["relw_in"], 16)
                sp.dma_start(relW[p:p + D, RO:RO + D], loopw).then_inc(m["relw_in"], 16)
            sp.dma_start(src_sb, src.rearrange("(p e) -> p e", p=PN)).then_inc(m["edges_in"], 16)
            sp.dma_start(et_sb, etype.rearrange("(p e) -> p e", p=PN)).then_inc(m["edges_in"], 16)
            sp.dma_start(srcp_d[0:E].rearrange("(a b) -> a b", b=250), src.rearrange("(a b) -> a b", b=250)).then_inc(m["srcp_out"], 16)
            for j, (wt, bias) in enumerate(((wattn, battn), (wmsg, bmsg))):
                sp.dma_start(wraw[0:D, j * IO:(j + 1) * IO], wt).then_inc(m["wraw_in"], 16)
                sp.dma_start(wraw[D:D + 1, j * IO:(j + 1) * IO], bias.rearrange("(a c) -> a c", a=1)).then_inc(m["wraw_in"], 16)
            sp.dma_start(srcp_d[E:E + S].rearrange("(a b) -> a b", a=1), padrow[:, 0:S].bitcast(I32)).then_inc(m["pad_out"], 16)
            sp.dma_start(pairp_d[E:E + S].rearrange("(a b) -> a b", a=1), padrow[:, 0:S].bitcast(I32)).then_inc(m["pad_out"], 16)
            sp.dma_start(efp_d[E * D:(E + S) * D].rearrange("(a b) -> a b", a=1), padrow).then_inc(m["pad_out"], 16)
            sp.dma_start(h2_d[N:N + 1, :], pad1[:]).then_inc(m["pad_out"], 16)
            rows = table_d.rearrange("(p c r) d -> p c (r d)", p=PN, c=C)
            with sp.Fori(0, C // 2) as t:
                for j in range(2):
                    sp.wait_ge(m["tbl_sb"], t * 8 + (4 * j + 4 + 2))
                    for a, b in ((0, 112), (112, PN)):
                        sp.dma_start(rows[a:b, ds(2 * t + j, 1), :].rearrange("p a n -> p (a n)"),
                                     tbl[a:b, j, :]).then_inc(m[f"tbl_out{j}"], 16)
            sp.dma_start(efp_d[0:E * D].rearrange("(a b) -> a b", b=1375),
                         efeat.rearrange("e d -> (e d)").rearrange("(a b) -> a b", b=1375)).then_inc(m["efp_out"], 16)
            sp.wait_ge(m["wsplit"], 1)
            for j, part in enumerate((0, 1, 2, 0, 1, 0)):
                sp.dma_start(wst[j * D:(j + 1) * D, :], wparts[0:D, part, :]).then_inc(m["wts_in"], 16)
            for part in range(3):
                sp.dma_start(wst[6 * D + part:6 * D + part + 1, :], wparts[D:D + 1, part, :]).then_inc(m["wts_in"], 16)
            sp.dma_start(wst[KE - 1:KE, :], urow[:]).then_inc(m["wts_in"], 16)
            sp.wait_ge(m["efp_out"], 16)
            sp.wait_ge(m["wts_in"], 16 * 10)

        @block.gpsimd
        def _(pool):
            pool.memset(ident[:], 0.0).then_inc(m["init"], 1)
            pool.memset(tri[:], 1.0).then_inc(m["init"], 1)
            pool.iota(nodei[:], [[1, C + 1]], base=0, channel_multiplier=C).then_inc(m["init"], 1)
            pool.iota(iotai[:], [[1, S]], base=0, channel_multiplier=0).then_inc(m["init"], 1)
            pool.wait_ge(m["init"], 4)
            pool.affine_select(out=ident[:], in_=ident[:], compare_op=ALU.not_equal, fill=1.0, base=0,
                               pattern=[[-1, 128]], channel_multiplier=1).then_inc(m["const"], 1)
            pool.affine_select(out=tri[:], in_=tri[:], compare_op=ALU.is_ge, fill=0.0, base=0,
                               pattern=[[1, C]], channel_multiplier=-1).then_inc(m["const"], 1)
            pool.wait_ge(m["firsts_ready"], 1)
            pool.dma_start(first_d.rearrange("(p c) -> p c", p=PN), firsts[:]).then_inc(m["firsts_dram"], 16)
            pool.wait_ge(m["firsts_dram"], 16)
            pool.dma_start(firstrow, first_d.rearrange("(a c) -> a c", a=1).to_broadcast([PN, NROW])).then_inc(m["firstrow_in"], 16)
            pool.wait_ge(m["rows_ready"], 1)
            for c in range(C + 1):
                pool.indirect_dma_start(out=dstblk[:, c, :], out_offset=None, in_=dst.rearrange("(r w) -> r w", w=ROW),
                                        in_offset=bass.IndirectOffsetOnAxis(ap=rowi[:, c:c + 1].bitcast(U32), axis=0)).then_inc(m["rows_in"], 16)
            pool.wait_ge(m["pair_ready"], 1)
            pool.dma_start(pairp_d[0:E].rearrange("(p e) -> p e", p=PN), pair_sb).then_inc(m["pair_out"], 16)
            pool.wait_ge(m["key_ready"], 1)
            pool.dma_start(key_d.rearrange("(p c) -> p c", p=PN), key[:]).then_inc(m["key_dram"], 16)
            pool.wait_ge(m["key_dram"], 16)
            pool.dma_start(keyrow, key_d.rearrange("(a c) -> a c", a=1).to_broadcast([PN, N])).then_inc(m["keyrow_in"], 16)
            pool.wait_ge(m["rec_ready"], 1)
            for c in range(C):
                pool.indirect_dma_start(out=info_d, out_offset=bass.IndirectOffsetOnAxis(ap=ranki[:, c:c + 1].bitcast(U32), axis=0),
                                        in_=rec[:, c, :], in_offset=None).then_inc(m["info_dram"], 16)
            pool.wait_ge(m["info_dram"], 16 * C)
            for a in (0, C // 2):
                pool.dma_start(info[:, a:a + C // 2, :],
                               info_d[a * PN:(a + C // 2) * PN, :].rearrange("(g p) w -> p g w", p=PN)).then_inc(m["info_in"], 16)

            pool.iota(winint, [[1, NW]], base=0, channel_multiplier=0).then_inc(m["win_iota"], 1)
            pool.wait_ge(m["win_ready"], 16)
            pairs = pool.value_load(npair[0:1, 0:1], min_val=C // 2, max_val=NW // 2 - 2)
            pool.wait_ge(m["tbl_out0"], 2 * 16 * (C // 2))
            pool.wait_ge(m["tbl_out1"], 2 * 16 * (C // 2))
            pool.wait_ge(m["pair_out"], 16)
            pool.wait_ge(m["pad_out"], 16 * 4)
            cum = [pool.alloc_register("cumP0"), pool.alloc_register("cumP1")]
            for r in cum:
                pool.reg_mov(r, 0)

            def pair_block(w, q):
                pool.wait_ge(m["bst_ready"], w + 1)
                pool.sem_inc(m["passed"], 1)
                pool.indirect_dma_start(out=blkidx[:, q, :], out_offset=None, in_=pairp_d.rearrange("(e a) -> e a", a=1),
                                        in_offset=bass.IndirectOffsetOnAxis(ap=bst[:, q:q + 1].bitcast(U32), axis=0)).then_inc(m["blk_in"], 16)

            def gather(rows, idx, q, b, done):
                for s in range(b * BLK, (b + 1) * BLK):
                    pool.indirect_dma_start(out=gath[:, q, s, :], out_offset=None, in_=rows,
                                            in_offset=bass.IndirectOffsetOnAxis(ap=idx[:, q, s:s + 1].bitcast(U32), axis=0)).then_inc(done[q], 16)

            pair_block(0, 0)
            with pool.Fori(0, pairs) as i:
                for q in range(2):
                    k = 2 * i + q
                    _, nb = window(pool, k)
                    pool.wait_ge(m["blk_in"], 16 * k + 16)
                    pool.wait_ge(m["l0_math"], k + 1)
                    pool.sem_inc(m["passed"], 1)
                    for b in range(MINB):
                        gather(table_d, blkidx, q, b, tgath)
                    if q:
                        pool.wait_ge(tgath[0], pool.snap(cum[0]) * 96)
                        pool.sem_inc(m["passed"], 1)
                    else:
                        with pool.If(i > 0):
                            pool.wait_ge(tgath[1], pool.snap(cum[1]) * 96)
                            pool.sem_inc(m["passed"], 1)
                    pair_block(k + 1, 1 - q)
                    for b in range(MINB, NBW):
                        with pool.If(nb > b):
                            gather(table_d, blkidx, q, b, tgath)
                    pool.reg_add(cum[q], cum[q], nb)
            pool.wait_ge(m["blk_in"], pairs * 32 + 16)
            pool.sem_inc(m["passed"], 1)
            pool.wait_ge(m["h2_ready"], 1)
            for c in range(C):
                pool.indirect_dma_start(out=h2_d, out_offset=bass.IndirectOffsetOnAxis(ap=nidx[:, c:c + 1].bitcast(U32), axis=0),
                                        in_=h2[:, c, :], in_offset=None).then_inc(m["h2_out"], 16)
            pool.wait_ge(m["srcp_out"], 16)
            pool.wait_ge(m["efp_out"], 16)

            def edge_block(w, q):
                pool.wait_ge(m["bst1_ready"], w + 1)
                pool.wait_ge(m["raw_free"], w + 1)
                pool.sem_inc(m["passed"], 1)
                off = bass.IndirectOffsetOnAxis(ap=bst[:, q:q + 1].bitcast(U32), axis=0)
                pool.indirect_dma_start(out=blkidx[:, q, :], out_offset=None, in_=srcp_d.rearrange("(e a) -> e a", a=1),
                                        in_offset=off).then_inc(m["src_in"], 16)
                pool.indirect_dma_start(out=efraw[:, 0, 0:S * D], out_offset=None, in_=efp_d.rearrange("(e d) -> e d", d=D),
                                        in_offset=off).then_inc(m["ef_in"], 16)

            sent = pool.alloc_register("sent")
            pool.reg_mov(sent, 0)

            def scatter(q):
                w = pool.snap(sent)
                pool.wait_ge(m["fin"], w + 1)
                pool.sem_inc(m["passed"], 1)
                with pool.If(w > 0):
                    pool.wait_ge(m["out_done"], w * 16)
                    pool.sem_inc(m["passed"], 1)
                pool.indirect_dma_start(out=out, out_offset=bass.IndirectOffsetOnAxis(ap=oidx[:, q:q + 1].bitcast(U32), axis=0),
                                        in_=orow[:, q, :], in_offset=None, bounds_check=N - 1, oob_is_err=False).then_inc(m["out_done"], 16)
                pool.reg_add(sent, sent, 1)

            edge_block(0, 0)
            pool.wait_ge(m["h2_out"], 16 * C)
            with pool.Fori(0, pairs) as i:
                for q in range(2):
                    k = 2 * i + q
                    _, nb = window(pool, k)
                    pool.wait_ge(m["idx_ready"], k + 1)
                    edge_block(k + 1, 1 - q)
                    pool.wait_ge(m["h_free"], k + 1)
                    pool.sem_inc(m["passed"], 1)
                    for b in range(MINB):
                        gather(h2_d, hidx, q, b, hgath)
                    for b in range(MINB, NBW):
                        with pool.If(nb > b):
                            gather(h2_d, hidx, q, b, hgath)
                    with pool.If(i > 0):
                        scatter(q)
            for q in range(2):
                scatter(q)
            pool.wait_ge(m["out_done"], pairs * 32)

        @block.tensor
        def _(pe):
            pe.wait_ge(m["const"], 2)
            pe.wait_ge(m["htan_ready"], 1)
            for t in range(C // 2):
                if t >= 12 and t % 4 == 0:
                    pe.wait_ge(m["hT_sb"], t // 4 - 2)
                last = nc.tensor.transpose(psT[0:64, t % 12, 0:PN], htan32[:, 2 * t:2 * t + 2, :].rearrange("p c k -> p (c k)"),
                                           ident[0:PN, 0:PN])
                if t % 4 == 3 or t == C // 2 - 1:
                    last.then_inc(m["hT_ps"], 1)
            pe.wait_ge(m["relw_in"], 16 * 6)
            with pe.Fori(0, C // 2) as t:
                pe.wait_ge(m["hst_sb"], t + 1)
                for j in range(2):
                    for h in range(4):
                        u = 4 * j + h
                        pe.wait_ge(m["tbl_sb"], t * 8 + (u + 1))
                        for a in range(2):
                            c0 = (2 * h + a) * PIECE
                            n = PIECE + (D if h == 3 and a else 0)
                            last = nc.tensor.matmul(psW[0:PN, u % 2, 512 * a:512 * a + n],
                                                    hst[32 * j:32 * j + D + 1, :],
                                                    relW[32 * j:32 * j + D + 1, c0:c0 + n], start=True, stop=True)
                        last.then_inc(m["tbl_ps"], 1)
            pe.wait_ge(m["info_in"], 32)
            pe.wait_ge(m["hT_sb"], (C // 2 + 3) // 4)
            nc.tensor.transpose(psT[0:C, 0, 0:PN], info[:, 0:C, 2 * D + 1], ident[0:PN, 0:PN]).then_inc(m["deg_T"], 1)
            pe.wait_ge(m["plan_col"], 1)
            nc.tensor.matmul(psT[0:C, 4, 0:1], tri[:], col[:, 2:3], start=True, stop=True)
            nc.tensor.matmul(psT[0:PN, 8, 0:1], ones[:], col[:, 2:3], start=True, stop=True).then_inc(m["plan_ps"], 1)
            pe.wait_ge(m["plan_col"], 2)
            for t in range(NW // 512):
                pe.wait_ge(m["win_psfree"], t + 1)
                for j, rhs in ((0, winhot), (1, winhot), (2, winrel)):
                    last = nc.tensor.matmul(psT[0:PN, 4 * j:4 * j + 4, :].rearrange("p a n -> p (a n)"), lhs[:, j, :],
                                            rhs[:, 512 * t:512 * t + 512], start=True, stop=True)
                last.then_inc(m["win_ps"], 1)

            pe.wait_ge(m["win_ready"], 16)
            pairs = pe.value_load(npair[0:1, 0:1], min_val=C // 2, max_val=NW // 2 - 2)
            pe.wait_ge(m["wts_in"], 16 * 10)
            cumb, nbp = pe.alloc_register("cumBp"), pe.alloc_register("nbPrev")
            pe.reg_mov(cumb, 0)
            pe.reg_mov(nbp, 0)

            def transposes(w):
                pe.wait_ge(m["ef_ready"], w + 1)
                for t in range(S // 8):
                    pe.wait_ge(m["efT_sb"], w * (S // 8) + (t + 1))
                    for j in range(8):
                        last = nc.tensor.transpose(psTb[0:KE, t % 3, j, 0:PN], efs[:, 8 * t + j, :], identb[0:PN, 0:PN])
                    last.then_inc(m["efT_ps"], 1)

            def weights(c0, q, b, at0):
                for s in range(2):
                    pe.wait_ge(m["w_free"], at0 + (s + 1))
                    for j in range(3):
                        last = nc.tensor.matmul(psW[0:PN, s, j * IO:(j + 1) * IO], efT[:, q, b * BLK + 3 * s + j, 0:PN],
                                                wst[:, c0:c0 + IO], start=True, stop=True)
                    last.then_inc(m["w_ready"], 1)

            def exp_sums(q, b):
                for s in range(BLK):
                    nc.tensor.matmul(psS[0:PN, 0:IO], ident[0:PN, 0:PN], score[:, q, b * BLK + s, :], start=False, stop=False)

            def close_sums():
                nc.tensor.matmul(psS[0:PN, :], zero[:, 0:PN], zero[:], start=False, stop=True).then_inc(m["sum_done"], 1)

            transposes(0)
            with pe.Fori(0, pairs) as i:
                for q in range(2):
                    k = 2 * i + q
                    _, nb = window(pe, k)
                    tb, prev = pe.snap(cumb), pe.snap(nbp)
                    pe.wait_ge(m["efT_sb"], k * (S // 8) + (S // 8 + 3))
                    for b in range(NBW):
                        with pe.If(nb > b):
                            weights(0, q, b, tb * 4 + 2 * b)
                        with pe.If(prev > b):
                            exp_sums(1 - q, b)
                    with pe.If(prev > 0):
                        close_sums()
                    transposes(k + 1)
                    pe.wait_ge(m["sum_read"], k + 1)
                    nc.tensor.matmul(psS[0:PN, :], zero[:, 0:PN], zero[:], start=True, stop=False)
                    weights(IO, q, 0, tb * 4 + nb * 2)
                    for b in range(NBW):
                        if b + 1 < NBW:
                            with pe.If(nb > b + 1):
                                weights(IO, q, b + 1, tb * 4 + nb * 2 + (2 * b + 2))
                        with pe.If(nb > b):
                            pe.wait_ge(m["q_ready"], tb + (b + 1))
                            for s in range(BLK):
                                c0 = (b % RING) * BLK * IO + s * IO
                                last = nc.tensor.matmul(psS[0:PN, IO:2 * IO], ident[0:PN, 0:PN], prod[:, c0:c0 + IO],
                                                        start=False, stop=False)
                            last.then_inc(m["q_free"], 1)
                    pe.reg_add(cumb, cumb, nb)
                    pe.reg_mov(nbp, nb)
            prev = pe.snap(nbp)
            for b in range(NBW):
                with pe.If(prev > b):
                    exp_sums(1, b)
            close_sums()

        @block.scalar
        def _(act):
            act.wait_ge(m["var_ready"], 1)
            nc.scalar.activation(nrm[:, 1, :], nrm[:, 0, :], ACT.Sqrt).then_inc(m["std_ready"], 1)
            act.wait_ge(m["var_ready"], 2)
            nc.scalar.activation(nrm[:, 1, :], nrm[:, 0, :], ACT.Sqrt).then_inc(m["std_ready"], 1)
            for t in range(0, C // 2, 4):
                n = min(4, C // 2 - t)
                act.wait_ge(m["hT_ps"], t // 4 + 1)
                nc.scalar.copy(hT[:, t:t + n, 0:PN], psT[0:64, t % 12:t % 12 + n, 0:PN]).then_inc(m["hT_sb"], 1)
            act.wait_ge(m["hT_sb"], (C // 2 + 3) // 4)
            with act.Fori(0, C // 2) as t:
                nc.scalar.copy(hst[:], hT[:, ds(t, 1), 0:PN].rearrange("k a n -> k (a n)")).then_inc(m["hst_sb"], 1)
                for j in range(2):
                    with act.If(t > 0):
                        act.wait_ge(m[f"tbl_out{j}"], t * 32)
                        act.sem_inc(m["passed"], 1)
                    for h in range(4):
                        u = 4 * j + h
                        act.wait_ge(m["tbl_ps"], t * 8 + (u + 1))
                        if h == 3:
                            nc.scalar.copy(rec[:, ds(2 * t + j, 1), D:2 * D].rearrange("p a d -> p (a d)"),
                                           psW[0:PN, u % 2, 512 + PIECE:512 + PIECE + D]).then_inc(m["loop_ready"], 1)
                        nc.scalar.copy(tbl[:, j, 2 * h * PIECE:(2 * h + 2) * PIECE].rearrange("p (a n) -> p a n", a=2),
                                       psW[0:PN, u % 2, :].rearrange("p (a n) -> p a n", a=2)[:, :, 0:PIECE]).then_inc(m["tbl_sb"], 1)
            act.wait_ge(m["loop_n"], 1)
            nc.scalar.activation(nrm[:, 3, :], nrm[:, 2, :], ACT.Sqrt).then_inc(m["loop_t"], 1)
            act.wait_ge(m["loop_t"], 1)
            nc.scalar.activation(nrm[:, 4, :], nrm[:, 3, :], ACT.Tanh, scale=SQC).then_inc(m["loop_t"], 1)

            act.wait_ge(m["tab_ready"], 1)
            act.dma_start(tabgn, tabtmp).then_inc(m["win_ready"], 16)
            act.wait_ge(m["win_ready"], 16)
            pairs = act.value_load(npair[0:1, 0:1], min_val=C // 2, max_val=NW // 2 - 2)
            with act.Fori(0, pairs) as i:
                for q in range(2):
                    k = 2 * i + q
                    act.wait_ge(m["n2_ready"], k + 1)
                    nc.scalar.activation(sl[:, 2, :], sl[:, 1, :], ACT.Sqrt)
                    nc.scalar.drain()
                    nc.scalar.activation(sl[:, 3, :], sl[:, 2, :], ACT.Tanh, scale=SQC).then_inc(m["th_ready"], 1)
            act.wait_ge(m["hnorm"], 1)
            nc.scalar.activation(nrm[:, 1, :], nrm[:, 0, :], ACT.Sqrt).then_inc(m["hnorm_out"], 1)
            act.wait_ge(m["hnorm"], 2)
            nc.scalar.activation(nrm[:, 1, :], nrm[:, 0, :], ACT.Sqrt).then_inc(m["hnorm_out"], 1)
            act.wait_ge(m["hnorm"], 3)
            nc.scalar.activation(nrm[:, 1, :], nrm[:, 0, :], ACT.Sqrt).then_inc(m["hnorm_out"], 1)

            cumb = act.alloc_register("cumBa")
            act.reg_mov(cumb, 0)

            def split(w):
                act.wait_ge(m["ef_in"], 16 * w + 16)
                nc.scalar.copy(efs[:, :, HI:MID].rearrange("p s (t d) -> p s t d", d=D),
                               efin.unsqueeze(2).to_broadcast([PN, S, 3, D])).then_inc(m["hi_done"], 1)
                act.wait_ge(m["res_done"], w + 1)
                nc.scalar.copy(efs[:, :, MID:LO].rearrange("p s (t d) -> p s t d", d=D),
                               efres.unsqueeze(2).to_broadcast([PN, S, 2, D])).then_inc(m["mid_done"], 1)

            def copies(w, q):
                for t in range(S // 8):
                    act.wait_ge(m["efT_ps"], w * (S // 8) + (t + 1))
                    nc.scalar.copy(efT[:, q, 8 * t:8 * t + 8, 0:PN], psTb[0:KE, t % 3, :, 0:PN]).then_inc(m["efT_sb"], 1)

            split(0)
            copies(0, 0)
            with act.Fori(0, pairs) as i:
                for q in range(2):
                    k = 2 * i + q
                    split(k + 1)
                    copies(k + 1, 1 - q)
                    _, nb = window(act, k)
                    tb = act.snap(cumb)
                    act.wait_ge(m["d_ready"], k + 1)
                    nc.scalar.activation(cfac[:, q, :], diff[:, q, :], ACT.Exp).then_inc(m["c_ready"], 1)
                    with act.Fori(0, nb) as b:
                        act.wait_ge(m["sub_done"], tb + b + 1)
                        v = score[:, q, ds(b * BLK, BLK), :]
                        nc.scalar.activation(v, v, ACT.Exp).then_inc(m["exp_done"], 1)
                    act.reg_add(cumb, cumb, nb)

        @block.vector
        def _(dve):
            V = nc.vector
            for name, n in (("tbl_sb", 2), ("l0_math", 2), ("h_free", 2), ("efT_sb", 3), ("w_free", 2), ("q_free", RING), ("raw_free", 1),
                            ("sum_read", 1), ("win_psfree", 1)):
                dve.sem_inc(m[name], n)
            V.memset(stage[:, 0:5300], 0.0)
            V.memset(urow[:, 0:IO], -BIG)
            V.memset(urow[:, IO:2 * IO], 0.0)
            V.memset(pad1[:], 1.0)
            V.memset(gath[:], 0.0)
            V.memset(zero[:], 0.0)
            V.memset(ones[:], 1.0)
            V.memset(info[:], 0.0)
            V.memset(npad[:], float(N))
            V.memset(lamsum[:], 0.0)
            V.memset(work[:], 0.0)
            V.memset(xnew[:], 0.0)
            V.drain().then_inc(m["wzero"], 1)

            def row_sum(o, i):
                V.tensor_reduce(o, i, AX.X, ALU.add)
                V.drain()

            def tt(o, a, b, op):
                V.tensor_tensor(o, a, b, op)
                V.drain()

            def ts(o, a, s1, s2, op0, op1=None):
                if op1 is None:
                    V.tensor_scalar(o, a, s1, None, op0)
                else:
                    V.tensor_scalar(o, a, s1, s2, op0, op1)
                V.drain()

            def norm_relu(o, i, t0, to_act, from_act, n):
                row_sum(nrm[:, 2, :], i)
                ts(nrm[:, 2, :], nrm[:, 2, :], 1.0 / D, None, ALU.mult)
                tt(t0, i, bc(nrm[:, 2, :], D), ALU.subtract)
                tt(o, t0, t0, ALU.mult)
                row_sum(nrm[:, 2, :], o)
                V.tensor_scalar(nrm[:, 0, :], nrm[:, 2, :], 1.0 / D, LN_EPS, ALU.mult, ALU.add).then_inc(to_act, 1)
                dve.wait_ge(from_act, n)
                V.reciprocal(nrm[:, 2, :], nrm[:, 1, :])
                V.drain()
                tt(t0, t0, bc(nrm[:, 2, :], D), ALU.mult)
                ts(o, t0, 0.0, None, ALU.max)

            dve.wait_ge(m["x_in"], 16)
            h, t0, t1 = tmp(0), tmp(1), tmp(2)
            norm_relu(h, rec[:, :, 0:D], t0, m["var_ready"], m["std_ready"], 1)
            tt(t0, h, h, ALU.mult)
            row_sum(nrm[:, 2, :], t0)
            V.tensor_scalar(nrm[:, 0, :], nrm[:, 2, :], MIN_NORM, None, ALU.max).then_inc(m["var_ready"], 1)
            dve.wait_ge(m["std_ready"], 2)
            z, z2, acc = nrm[:, 2, :], nrm[:, 3, :], nrm[:, 4, :]
            ts(z, nrm[:, 1, :], SQC, 1.0 - BALL, ALU.mult, ALU.min)
            tt(z2, z, z, ALU.mult)
            ts(acc, z2, 1.0 / 23, 1.0 / 21, ALU.mult, ALU.add)
            for n in range(19, 0, -2):
                tt(acc, acc, z2, ALU.mult)
                ts(acc, acc, 1.0 / n, None, ALU.add)
            tt(t0, h, bc(acc, D), ALU.mult)
            V.memset(htan32[:, :, D:D + 1], 1.0)
            V.tensor_copy(htan32[:, :, 0:D], t0)
            V.drain().then_inc(m["htan_ready"], 1)

            dve.wait_ge(m["dst_in"], 16)
            V.tensor_copy(firsts[:], dst_sb.rearrange("p (r w) -> p r w", w=ROW)[:, :, 0]).then_inc(m["firsts_ready"], 1)
            dve.wait_ge(m["const"], 2)
            V.tensor_copy(identb[:], ident[:])
            V.tensor_copy(nodeid[:], nodei[:])
            V.tensor_copy(iotaf[:], iotai[:])
            V.drain()
            dve.wait_ge(m["firstrow_in"], 16)
            for c in range(C + 1):
                V.tensor_scalar(junk[:, 0:NROW], firstrow, nodeid[:, c:c + 1], 0.0, ALU.is_lt, ALU.add,
                                accum_out=cnt[:, c:c + 1])
                V.drain()
            ts(cnt[:], cnt[:], -1.0, 0.0, ALU.add, ALU.max)
            V.tensor_copy(rowi[:], cnt[:]).then_inc(m["rows_ready"], 1)
            dve.wait_ge(m["edges_in"], 32)
            V.scalar_tensor_tensor(pair_sb, src_sb, float(R), et_sb, ALU.mult, ALU.add).then_inc(m["pair_ready"], 1)
            dve.wait_ge(m["rows_in"], 16 * (C + 1))
            tt(less, dstblk, bc(nodeid[:], ROW), ALU.is_lt)
            row_sum(start0[:], less)
            V.scalar_tensor_tensor(start0[:], cnt[:], float(ROW), start0[:], ALU.mult, ALU.add)
            V.drain()
            tt(rec[:, :, 2 * D + 1], start0[:, 1:C + 1], start0[:, 0:C], ALU.subtract)
            V.tensor_copy(rec[:, :, 2 * D], start0[:, 0:C])
            V.tensor_copy(rec[:, :, 2 * D + 2], nodeid[:, 0:C])
            V.memset(rec[:, :, 2 * D + 3:2 * D + 4], 0.0)
            ts(key[:], rec[:, :, 2 * D + 1], 1023.0, 8192.0, ALU.min, ALU.mult)
            V.scalar_tensor_tensor(key[:], nodeid[:, 0:C], -1.0, key[:], ALU.mult, ALU.add).then_inc(m["key_ready"], 1)
            dve.wait_ge(m["keyrow_in"], 16)
            for c in range(C):
                V.tensor_scalar(junk, keyrow, key[:, c:c + 1], 0.0, ALU.is_gt, ALU.add, accum_out=rank[:, c:c + 1])
                V.drain()
            V.tensor_copy(ranki[:], rank[:])
            dve.wait_ge(m["loop_ready"], C)
            lp = rec[:, :, D:2 * D]
            tt(t0, lp, lp, ALU.mult)
            row_sum(nrm[:, 2, :], t0)
            V.tensor_scalar(nrm[:, 2, :], nrm[:, 2, :], MIN_NORM, None, ALU.max)
            V.drain().then_inc(m["loop_n"], 1)
            dve.wait_ge(m["loop_t"], 2)
            ts(nrm[:, 3, :], nrm[:, 3, :], SQC, None, ALU.mult)
            V.reciprocal(nrm[:, 5, :], nrm[:, 3, :])
            V.drain()
            tt(nrm[:, 4, :], nrm[:, 4, :], nrm[:, 5, :], ALU.mult)
            tt(lp, lp, bc(nrm[:, 4, :], D), ALU.mult)
            V.drain().then_inc(m["rec_ready"], 1)

            dve.wait_ge(m["deg_T"], 1)
            V.tensor_reduce(col[:, 0:1], psT[0:C, 0, 0:PN], AX.X, ALU.max)
            V.drain()
            MAGIC = 8388608.0

            def ceil_div(o, i, n):
                ts(o, i, 1.0, None, ALU.max)
                ts(o, o, (n - 1) / 2.0, 1.0 / n, ALU.add, ALU.mult)
                ts(o, o, MAGIC, None, ALU.add)
                ts(o, o, -MAGIC, None, ALU.add)

            ceil_div(col[:, 1:2], col[:, 0:1], BLK)
            ceil_div(col[:, 2:3], col[:, 1:2], NBW)
            V.drain().then_inc(m["plan_col"], 1)
            dve.wait_ge(m["plan_ps"], 1)
            V.tensor_copy(col[:, 3:4], psT[0:C, 4, 0:1])
            V.tensor_copy(npairf[:], psT[0:PN, 8, 0:1])
            V.drain()
            tt(col[:, 4:5], col[:, 3:4], col[:, 2:3], ALU.subtract)
            ts(npairf[:], npairf[:], 0.5, 0.25, ALU.mult, ALU.add)
            ts(npairf[:], npairf[:], MAGIC, None, ALU.add)
            ts(npairf[:], npairf[:], -MAGIC, None, ALU.add)
            V.tensor_copy(npair[:], npairf[:])
            dve.wait_ge(m["win_iota"], 1)
            V.tensor_copy(winpos, winint)
            V.drain()
            V.tensor_scalar(winrel, winpos, col[:, 3:4], None, ALU.is_ge)
            V.drain()
            V.scalar_tensor_tensor(winhot, winpos, col[:, 4:5], winrel, ALU.is_ge, ALU.subtract)
            V.drain()
            V.scalar_tensor_tensor(winrel, winpos, col[:, 4:5], winhot, ALU.subtract, ALU.mult)
            ts(col[:, 5:6], nodeid[0:C, 0:1], 1.0 / C, None, ALU.mult)
            ts(col[:, 5:6], col[:, 5:6], MAGIC, None, ALU.add)
            ts(col[:, 5:6], col[:, 5:6], -MAGIC, None, ALU.add)
            ts(col[:, 5:6], col[:, 5:6], -float(C), None, ALU.add)
            for j, cc in ((0, 5), (1, 1)):
                ts(lhs[:, j, :], ones[:], col[:, cc:cc + 1], None, ALU.mult)
            V.tensor_copy(lhs[:, 2, :], ones[:])
            V.drain().then_inc(m["plan_col"], 1)
            wv = wvt
            for t in range(NW // 512):
                dve.wait_ge(m["win_ps"], t + 1)
                pg, pn, pr = (psT[0:PN, 4 * j:4 * j + 4, :].rearrange("p a n -> p (a n)") for j in range(3))
                V.tensor_copy(tabs[0:PN, 512 * t:512 * t + 512], pr)
                V.tensor_copy(wv[:, 0, :], pr)
                V.drain()
                V.scalar_tensor_tensor(wv[:, 0, :], wv[:, 0, :], -float(NBW), pn, ALU.mult, ALU.add)
                V.tensor_scalar(wv[:, 1, :], pg, float(NBW), float(NBW * C - 1), ALU.mult, ALU.add)
                V.drain().then_inc(m["win_psfree"], 1)
                ts(wv[:, 0, :], wv[:, 0, :], float(NBW), float(MINB), ALU.min, ALU.max)
                tt(tabtmp[:, 512 * t:512 * t + 512], wv[0:1, 1, :], wv[0:1, 0, :], ALU.add)
            V.tensor_copy(nidx[:, 0:C], info[:, 0:C, 2 * D + 2])
            V.tensor_copy(nidx[:, C:C + 1], npad[:])
            V.memset(numer, 0.0)
            V.drain().then_inc(m["tab_ready"], 1)
            dve.wait_ge(m["wraw_in"], 16 * 4)
            V.tensor_copy(wparts[:, 0, :], wraw)
            V.drain()
            tt(wres, wraw, wparts[:, 0, :], ALU.subtract)
            V.tensor_copy(wparts[:, 1, :], wres)
            V.drain()
            V.tensor_tensor(wparts[:, 2, :], wres, wparts[:, 1, :], ALU.subtract)
            V.drain().then_inc(m["wsplit"], 1)
            dve.wait_ge(m["win_ready"], 16)
            pairs = dve.value_load(npair[0:1, 0:1], min_val=C // 2, max_val=NW // 2 - 2)

            start = info[:, :, 2 * D]
            deg = info[:, :, 2 * D + 1]

            def window_start(w, q, done):
                g, _ = window(dve, w)
                n = tabs[0:PN, ds(w, 1)]
                V.scalar_tensor_tensor(bstf[:, q:q + 1], n, float(S), start[:, ds(g, 1)], ALU.mult, ALU.add)
                V.scalar_tensor_tensor(rem[:, q:q + 1], n, -float(S), deg[:, ds(g, 1)], ALU.mult, ALU.add)
                V.tensor_scalar(keep[:, q:q + 1], n, 1.0, None, ALU.min)
                V.drain()
                V.tensor_scalar(keepbig[:, q:q + 1], keep[:, q:q + 1], -1.0, 2.0 * BIG, ALU.add, ALU.mult)
                V.tensor_scalar(bst[:, q:q + 1], bstf[:, q:q + 1], float(E), None, ALU.min)
                V.drain().then_inc(done, 1)

            cum = [dve.alloc_register("cumV0"), dve.alloc_register("cumV1")]
            for r in cum:
                dve.reg_mov(r, 0)
            window_start(0, 0, m["bst_ready"])
            with dve.Fori(0, pairs) as i:
                for q in range(2):
                    k = 2 * i + q
                    G = gath[:, q, :, :]
                    g, nb = window(dve, k)
                    dve.reg_add(cum[q], cum[q], nb)
                    V.tensor_scalar(valid[:, q, :], iotaf[:], rem[:, q:q + 1], None, ALU.is_lt)
                    if q:
                        dve.wait_ge(m["blk_in"], 16 * k)
                        dve.sem_inc(m["passed"], 1)
                    else:
                        with dve.If(i > 0):
                            dve.wait_ge(m["blk_in"], 16 * k)
                            dve.sem_inc(m["passed"], 1)
                    window_start(k + 1, 1 - q, m["bst_ready"])
                    dve.wait_ge(tgath[q], dve.snap(cum[q]) * 96)
                    tt(sq, G, G, ALU.mult)
                    row_sum(sl[:, 0, :], sq)
                    V.tensor_scalar(sl[:, 1, :], sl[:, 0, :], MIN_NORM, None, ALU.max).then_inc(m["n2_ready"], 1)
                    dve.wait_ge(m["th_ready"], k + 1)
                    ts(sl[:, 2, :], sl[:, 2, :], SQC, None, ALU.mult)
                    V.reciprocal(sl[:, 4, :], sl[:, 2, :])
                    V.drain()
                    tt(sl[:, 3, :], sl[:, 3, :], sl[:, 4, :], ALU.mult)
                    tt(sl[:, 4, :], sl[:, 3, :], sl[:, 3, :], ALU.mult)
                    tt(sl[:, 4, :], sl[:, 4, :], sl[:, 0, :], ALU.mult)
                    ts(sl[:, 4, :], sl[:, 4, :], -CURV, 1.0, ALU.mult, ALU.add)
                    ts(sl[:, 4, :], sl[:, 4, :], EPS, 0.5, ALU.add, ALU.mult)
                    V.reciprocal(sl[:, 5, :], sl[:, 4, :])
                    V.drain()
                    tt(sl[:, 5, :], sl[:, 5, :], valid[:, q, :], ALU.mult)
                    row_sum(lsum[:], sl[:, 5, :])
                    tt(sl[:, 3, :], sl[:, 3, :], sl[:, 5, :], ALU.mult)
                    V.tensor_tensor(sq, G, bc(sl[:, 3, :], D), ALU.mult)
                    V.drain().then_inc(m["l0_math"], 1)
                    row_sum(nsum[:], sq.rearrange("p s d -> p d s"))
                    V.tensor_tensor(numer[:, ds(g, 1), :].rearrange("p a d -> p (a d)"),
                                    numer[:, ds(g, 1), :].rearrange("p a d -> p (a d)"), nsum[:], ALU.add)
                    V.tensor_tensor(lamsum[:, ds(g, 1)], lamsum[:, ds(g, 1)], lsum[:], ALU.add)
                    V.drain()

            A, B, T = tmp(0), tmp(1), tmp(2)
            X0, Y = info[:, 0:C, 0:D], info[:, 0:C, D:2 * D]
            n0, n1, n2, n3, n4, n5 = (nrm[:, j, :] for j in (2, 3, 4, 5, 6, 7))
            V.tensor_scalar(nrm[:, 0, :], deg[:, 0:C], 1.0, None, ALU.max).then_inc(m["hnorm"], 1)
            dve.wait_ge(m["hnorm_out"], 1)
            V.reciprocal(n0, nrm[:, 1, :])
            V.drain()
            tt(n1, n0, deg[:, 0:C], ALU.mult)
            ts(n1, n1, EPS, None, ALU.add)
            V.reciprocal(n2, n1)
            V.drain()
            tt(n0, n0, n2, ALU.mult)
            tt(n1, n0, lamsum[:, 0:C], ALU.mult)
            ts(n1, n1, EPS, None, ALU.add)
            V.reciprocal(n2, n1)
            V.drain()
            tt(n0, n0, n2, ALU.mult)
            tt(A, numer[:, 0:C, :], bc(n0, D), ALU.mult)
            tt(T, A, A, ALU.mult)
            row_sum(n0, T)
            V.tensor_scalar(nrm[:, 0, :], n0, MIN_NORM, None, ALU.max).then_inc(m["hnorm"], 1)
            dve.wait_ge(m["hnorm_out"], 2)
            V.reciprocal(n1, nrm[:, 1, :])
            V.drain()
            ts(n1, n1, (1.0 - BALL) / SQC, 1.0, ALU.mult, ALU.min)
            tt(A, A, bc(n1, D), ALU.mult)
            tt(T, A, A, ALU.mult)
            row_sum(n0, T)
            tt(T, Y, Y, ALU.mult)
            row_sum(n1, T)
            tt(T, A, Y, ALU.mult)
            row_sum(n2, T)
            ts(n3, n2, 2.0 * CURV, 1.0, ALU.mult, ALU.add)
            tt(n4, n0, n1, ALU.mult)
            V.scalar_tensor_tensor(n4, n4, CURV * CURV, n3, ALU.mult, ALU.add)
            V.scalar_tensor_tensor(n3, n1, CURV, n3, ALU.mult, ALU.add)
            V.drain()
            ts(n4, n4, MIN_NORM, None, ALU.max)
            V.reciprocal(n5, n4)
            ts(n0, n0, -CURV, 1.0, ALU.mult, ALU.add)
            tt(T, A, bc(n3, D), ALU.mult)
            tt(B, Y, bc(n0, D), ALU.mult)
            tt(T, T, B, ALU.add)
            tt(T, T, bc(n5, D), ALU.mult)
            tt(xnew[:, 0:C, :], X0, T, ALU.add)
            norm_relu(h2, xnew[:, 0:C, :], tmp(3), m["hnorm"], m["hnorm_out"], 3)
            V.drain().then_inc(m["h2_ready"], 1)

            V.memset(mnew, 0.0)
            V.memset(total, 0.0)
            V.drain()
            sent = dve.alloc_register("sentV")
            dve.reg_mov(sent, 0)
            cumb = dve.alloc_register("cumBv")
            dve.reg_mov(cumb, 0)
            for r in cum:
                dve.reg_mov(r, 0)

            def edge_ids(w, q):
                dve.wait_ge(m["src_in"], 16 * w + 16)
                ts(valid[:, q, :], iotaf[:], rem[:, q:q + 1], None, ALU.is_lt)
                V.scalar_tensor_tensor(valid2[:], blkidx[:, q, :], -float(N), valid[:, q, :], ALU.add, ALU.mult)
                V.drain()
                V.tensor_scalar(hidx[:, q, :], valid2[:], float(N), None, ALU.add)
                V.drain().then_inc(m["idx_ready"], 1)

            def edge_residue(w):
                dve.wait_ge(m["hi_done"], w + 1)
                V.tensor_tensor(efres, efin, efs[:, :, HI:HI + D], ALU.subtract)
                V.drain().then_inc(m["res_done"], 1)
                dve.sem_inc(m["raw_free"], 1)

            def edge_last(w, q):
                V.tensor_copy(efs[:, :, 6 * D:6 * D + 3], bc(valid[:, q, :], 3))
                V.tensor_scalar(efs[:, :, KE - 1], valid[:, q, :], -1.0, 1.0, ALU.mult, ALU.add)
                dve.wait_ge(m["mid_done"], w + 1)
                V.tensor_tensor(efs[:, :, LO:LO + D], efres, efs[:, :, MID:MID + D], ALU.subtract)
                V.drain().then_inc(m["ef_ready"], 1)

            def finish(q, n):
                dve.wait_ge(m["c_ready"], n)
                tt(total, total, cfac[:, q, :].unsqueeze(1).to_broadcast([PN, 2, IO]), ALU.mult)
                dve.wait_ge(m["sum_done"], n)
                V.tensor_tensor(total, total, psS[0:PN, :].rearrange("p (a c) -> p a c", a=2), ALU.add)
                V.drain().then_inc(m["sum_read"], 1)
                V.reciprocal(ratio, total[:, 0, :])
                V.drain()
                tt(ratio, ratio, total[:, 1, :], ALU.mult)
                row_sum(ft[:], ratio.rearrange("p (i o) -> p o i", o=D))
                V.scalar_tensor_tensor(orow[:, q, :], ft[:], gx[:, q, D:D + 1], gx[:, q, 0:D], ALU.mult, ALU.add)
                V.tensor_copy(oidx[:, q:q + 1], gid[:, q:q + 1])
                V.drain().then_inc(m["fin"], 1)

            def row_free():
                dve.reg_add(sent, sent, 16)
                dve.wait_ge(m["out_done"], dve.snap(sent))
                dve.sem_inc(m["passed"], 1)

            dve.wait_ge(m["blk_in"], pairs * 32 + 16)
            dve.sem_inc(m["passed"], 1)
            window_start(0, 0, m["bst1_ready"])
            window_start(1, 1, m["bst1_ready"])
            edge_ids(0, 0)
            edge_residue(0)
            edge_last(0, 0)
            with dve.Fori(0, pairs) as i:
                for q in range(2):
                    k = 2 * i + q
                    edge_ids(k + 1, 1 - q)
                    g, nb = window(dve, k)
                    tb = dve.snap(cumb)
                    dve.reg_add(cum[q], cum[q], nb)
                    V.tensor_scalar(mold, mnew[:, 1 - q, :], keep[:, q:q + 1], keepbig[:, q:q + 1], ALU.mult, ALU.add)
                    V.tensor_copy(gx[:, q, 0:D], xnew[:, ds(g, 1), :].rearrange("p a d -> p (a d)"))
                    V.tensor_scalar(gx[:, q, D:D + 1], deg[:, ds(g, 1)], 1.0, None, ALU.min)
                    V.tensor_copy(gid[:, q:q + 1], nidx[:, ds(g, 1)])
                    V.drain()
                    window_start(k + 2, q, m["bst1_ready"])
                    dve.wait_ge(hgath[q], dve.snap(cum[q]) * 96)

                    def times_h(dst_ap, b, s, at0):
                        dve.wait_ge(m["w_ready"], at0 + (s + 1))
                        hb = gath[:, q, ds(b * BLK + 3 * s, 3), :]
                        V.tensor_tensor(dst_ap.rearrange("p s (i o) -> p s i o", o=D),
                                        psW[0:PN, s, 0:3 * IO].rearrange("p (s i o) -> p s i o", i=D, o=D),
                                        bc(hb, D), ALU.mult).then_inc(m["w_free"], 1)

                    def scores(b):
                        for s in range(2):
                            times_h(score[:, q, ds(b * BLK + 3 * s, 3), :], b, s, tb * 4 + b * 2)
                        V.drain()

                    scores(0)
                    edge_residue(k + 1)
                    scores(1)
                    V.tensor_tensor(macc, score[:, q, 0:BLK, :], score[:, q, BLK:2 * BLK, :], ALU.max)
                    edge_last(k + 1, 1 - q)
                    with dve.Fori(2, nb) as b:
                        scores(b)
                        V.tensor_tensor(macc, macc, score[:, q, ds(b * BLK, BLK), :], ALU.max)
                    V.drain()
                    V.tensor_reduce(mred, macc.rearrange("p s c -> p c s"), AX.X, ALU.max)
                    V.drain()
                    tt(mnew[:, q, :], mred, mold, ALU.max)
                    V.tensor_tensor(diff[:, q, :], mold, mnew[:, q, :], ALU.subtract).then_inc(m["d_ready"], 1)

                    if q:
                        with dve.If(i > 0):
                            row_free()
                        finish(0, k)
                    else:
                        with dve.If(i > 1):
                            row_free()
                        with dve.If(i > 0):
                            finish(1, k)

                    with dve.Fori(0, nb) as b:
                        blk = score[:, q, ds(b * BLK, BLK), :]
                        V.tensor_tensor(blk, blk, mnew[:, q, :].unsqueeze(1).to_broadcast([PN, BLK, IO]),
                                        ALU.subtract).then_inc(m["sub_done"], 1)
                        dve.wait_ge(m["q_free"], tb + b + 1)
                        par = (b % RING) * (BLK * IO)
                        for s in range(2):
                            times_h(prod[:, ds(par + 3 * s * IO, 3 * IO)].rearrange("p (s c) -> p s c", c=IO), b, s,
                                    tb * 4 + nb * 2 + b * 2)
                        V.drain()
                        dve.wait_ge(m["exp_done"], tb + b + 1)
                        pr = prod[:, ds(par, BLK * IO)]
                        V.tensor_tensor(pr, pr, blk.rearrange("p s c -> p (s c)"), ALU.mult).then_inc(m["q_ready"], 1)
                    V.drain().then_inc(m["h_free"], 1)
                    dve.reg_add(cumb, cumb, nb)
            row_free()
            finish(1, pairs * 2)


_INS = ["x", "src", "dst", "edge_attr_16", "edge_type_230", "L0_gnn_rel_weight", "L0_gnn_loop_weight", "L0_gnn_rel_emb",
        "L1_gnn_W_msg", "L1_gnn_b_msg", "L1_gnn_W_attn", "L1_gnn_b_attn"]


def kernel(**inputs):
    import numpy as _np
    import concourse.bacc as _bacc
    from concourse.bass_utils import run_bass_kernel_spmd as _run

    nc = _bacc.Bacc("TRN2", target_bir_lowering=False, num_devices=1)
    arrays, args = {}, []
    for name in _INS:
        a = _np.ascontiguousarray(inputs[name])
        arrays[f"in_{name}"] = a
        args.append(nc.dram_tensor(f"in_{name}", a.shape, mybir.dt.from_np(a.dtype), kind="ExternalInput").ap())
    out = nc.dram_tensor("out_0", (N, D), F32, kind="ExternalOutput").ap()
    scratch = [nc.dram_tensor(n, s, t, kind="Internal").ap() for n, s, t in (
        ("table", (N * R, D), F32), ("srcp", (E + S,), I32), ("pairp", (E + S,), I32), ("efp", ((E + S) * D,), F32),
        ("h2_dram", (N + 1, D), F32), ("first_dram", (NROW,), F32), ("key_dram", (N,), F32), ("info_dram", (N, INFO), F32))]
    build(nc, *args, out, scratch)
    r = _run(nc, [arrays], core_ids=[0])
    return r.results[0]["out_0"]
```

```python
from contextlib import ExitStack

import concourse.bass as bass
from concourse import mybir

F32 = mybir.dt.float32
BF16 = mybir.dt.bfloat16
I32 = mybir.dt.int32
I16 = mybir.dt.int16
U32 = mybir.dt.uint32
ALU = mybir.AluOpType
ACT = mybir.ActivationFunctionType
AX = mybir.AxisListType
ds = bass.ds

N, D, E, R = 6250, 16, 206250, 230
PN = 125
C = N // PN
IO = D * D
BLK = 6
NBW = 8
S = BLK * NBW
MINB = 3
HALF = BLK // 2
NHW, MINH = 2 * NBW, 2 * MINB
NV = 128
KT = 6 * (D + 1)
TSTEP = 19
WCH = 512
NW = 9 * WCH
KE = 6 * D + 4
HI, MID, LO = 0, 3 * D, 5 * D
RING = 3
RO = R * D
PIECE = RO // 8
ROW = 110
NROW = E // ROW
RPP = NROW // PN
EPP = E // PN
INFO = 2 * D + 4

BIG = 2.0 ** 120
CURV = 0.01
SQC = 0.1
EPS = 1e-6
MIN_NORM = 1e-10
BALL = 1e-5
LN_EPS = 1e-5


def build(nc, x, src, dst, efeat, etype, relw, loopw, relemb, wmsg, bmsg, wattn, battn, out, scratch):
    table_d, srcp_d, pairp_d, efp_d, h2_d, first_d, info_d = scratch
    ctx = ExitStack()
    with ctx:
        def sb(name, shape, dt=F32):
            return ctx.enter_context(nc.sbuf_tensor(name, shape, dt))

        def sem(name):
            return ctx.enter_context(nc.semaphore(name))

        arena = sb("arena", [128, 2 * S * IO])

        def at(off, n, p=PN, dt=F32):
            v = arena[0:p, off:off + n]
            return v if dt is F32 else v.bitcast(dt)

        score = arena[0:PN, :].rearrange("p (q s c) -> p q s c", q=2, c=IO)
        tbl = at(0, 2 * RO).rearrange("p (q n) -> p q n", q=2)
        o = 2 * RO
        firstrow = at(o, NROW)
        dstblk = at(o + NROW, (C + 1) * ROW, dt=I32).rearrange("p (c w) -> p c w", w=ROW)
        dst_sb = at(o + NROW, EPP, dt=I32)
        onehot = at(o, NV * C).rearrange("p (v c) -> p v c", c=C)
        count = at(o + NV * C, NV * C).rearrange("p (v c) -> p v c", c=C)
        ncls, total_cls, base = (at(o + 2 * NV * C + j * NV, NV) for j in range(3))
        junk = at(o + NROW + (C + 1) * ROW, NROW)
        less = at(o + NROW + (C + 1) * ROW, (C + 1) * ROW).rearrange("p (c w) -> p c w", w=ROW)
        src_sb = at(17300, EPP, dt=I32)
        htan6 = at(18960, C * KT // 2).bitcast(BF16).rearrange("p (c j k) -> p c j k", j=6, k=D + 1)
        winint, winpos = at(o, WCH, C, I32), at(o + WCH, WCH, C)
        winhot, winrel = at(o + 2 * WCH, WCH, C), at(o + 3 * WCH, WCH, C)
        lhs = at(21200, 3 * PN, C).rearrange("p (j n) -> p j n", j=3)
        rec = at(22700, C * INFO).rearrange("p (c w) -> p c w", w=INFO)

        def tmp(i):
            return at(o + NROW + (C + 1) * ROW + i * C * D, C * D).rearrange("p (c d) -> p c d", d=D)

        stage = sb("stage", [128, RING * BLK * IO + S * KE // 2 + S * 126])
        prod = stage[0:PN, 0:RING * BLK * IO]
        o2 = RING * BLK * IO
        efs = stage[0:PN, o2:o2 + S * KE // 2].bitcast(BF16).rearrange("p (s k) -> p s k", k=KE)
        o2 += S * KE // 2
        efT = stage[0:KE, o2:o2 + S * 126].bitcast(BF16).rearrange("k (q s n) -> k q s n", q=2, n=126)
        tabtmp = stage[0:1, 4608:4608 + NW // 2].bitcast(I16)
        wraw, wres = stage[0:D + 1, 11100:11100 + 2 * IO], stage[0:D + 1, 11612:11612 + 2 * IO]
        wparts = stage[0:D + 1, 12124:12124 + 3 * IO].bitcast(BF16).rearrange("k (j n) -> k j n", j=3)
        relW = stage[0:D + 1, 0:RO + D]
        rparts = stage[0:D + 1, RO + D:RO + D + 3 * (RO + D) // 2].bitcast(BF16).rearrange("k (j n) -> k j n", j=3)
        relW6 = stage[0:KT, 9240:9240 + (RO + D) // 2].bitcast(BF16)
        numer = stage[0:PN, 0:(C + 1) * D].rearrange("p (c d) -> p c d", d=D)

        work = sb("work", [128, BLK * IO + 10 * IO])
        hT6 = work[0:KT, 0:C * 126 // 2].bitcast(BF16).rearrange("k (c n) -> k c n", n=126)
        sq = work[0:PN, 0:S * D].rearrange("p (s d) -> p s d", d=D)
        sl = work[0:PN, S * D:S * D + 6 * S].rearrange("p (j s) -> p j s", s=S)
        macc = work[0:PN, 0:BLK * IO].rearrange("p (s c) -> p s c", c=IO)

        def col256(j, n=1):
            return work[0:PN, BLK * IO + j * IO:BLK * IO + (j + n) * IO]

        mold, ratio = col256(0), col256(1)
        mred = ratio
        total = col256(2, 2).rearrange("p (a c) -> p a c", a=2)
        mnew = col256(4, 2).rearrange("p (q c) -> p q c", q=2)
        diff = col256(6, 2).rearrange("p (q c) -> p q c", q=2)
        cfac = col256(8, 2).rearrange("p (q c) -> p q c", q=2)

        gath = sb("gath", [PN, 2, S, D])
        efraw = sb("efraw", [PN, 2, max(S * D, EPP // 2)])
        et_sb = efraw[:, :, :].rearrange("p q n -> p (q n)")[:, 0:EPP].bitcast(I32)
        pair_sb = et_sb
        efin = efraw[:, 0, 0:S * D].rearrange("p (s d) -> p s d", d=D)
        efres = efraw[:, 1, 0:S * D].rearrange("p (s d) -> p s d", d=D)
        wst = sb("wst", [KE, 2 * IO], BF16)
        info = sb("info", [PN, C + 1, INFO])
        xnew = sb("xnew", [PN, C + 1, D])
        h2 = tmp(4)
        lamsum = sb("lamsum", [PN, C + 1])
        tabs = sb("tabs", [128, NW], I16)
        tabgn = tabs[127:128, :]
        ident = sb("ident", [128, 128])
        identb = sb("identb", [128, 128], BF16)
        tri = sb("tri", [PN, PN])
        ones = sb("ones", [PN, PN])
        zero = sb("zero", [1, 512], BF16)
        urow = sb("urow", [1, 2 * IO], BF16)
        pad1 = sb("pad1", [1, D])
        padrow = gath[0:1, 0, :, :].rearrange("p s d -> p (s d)")
        nodei = sb("nodei", [PN, C + 1], I32)
        nodeid = sb("nodeid", [PN, C + 1])
        iotai = sb("iotai", [PN, NV], I32)
        iotaf = sb("iotaf", [PN, NV])
        firsts = sb("firsts", [PN, RPP])
        cnt = sb("cnt", [PN, C + 1])
        rowi = sb("rowi", [PN, C + 1], I32)
        start0 = sb("start0", [PN, C + 1])
        key = sb("key", [PN, C])
        rank = sb("rank", [PN, C])
        ranki = sb("ranki", [PN, C], I32)
        nidx = sb("nidx", [PN, C + 1], I32)
        col = sb("col", [C, 8])
        npairf = sb("npairf", [PN, 1])
        npair = sb("npair", [PN, 1], I32)
        nrm = sb("nrm", [PN, 8, C])
        bstf = sb("bstf", [PN, 2])
        bst = sb("bst", [PN, 2], I32)
        rem = sb("rem", [PN, 2])
        keep = sb("keep", [PN, 2])
        keepbig = sb("keepbig", [PN, 2])
        blkidx = sb("blkidx", [PN, 2, S], I32)
        hidx = sb("hidx", [PN, 2, S], I32)
        valid = sb("valid", [PN, 2, S])
        wv = work[0:PN, 0:2 * WCH].rearrange("p (a n) -> p a n", a=2)
        valid2 = sb("valid2", [PN, S])
        npad = sb("npad", [PN, 1])
        lsum = sb("lsum", [PN, 1])
        nsum = sb("nsum", [PN, D])
        gx = sb("gx", [PN, 2, D + 1])
        gid = sb("gid", [PN, 2], I32)
        orow = sb("orow", [PN, 2, D])
        oidx = sb("oidx", [PN, 2], I32)
        ft = sb("ft", [PN, D])

        psW = ctx.enter_context(nc.psum_tensor("psW", [128, 2, 1024], F32))
        psS = ctx.enter_context(nc.psum_tensor("psS", [128, 512], F32))
        psT = ctx.enter_context(nc.psum_tensor("psT", [128, 12, 128], F32))
        psTb = psT[:, :, :].rearrange("p a n -> p (a n)").bitcast(BF16).rearrange("p (t s n) -> p t s n", t=3, n=128)

        names = ("x_in dst_in edges_in relw_in wts_in wzero pads_ready const var_ready std_ready htan_ready hT_ps hT_sb "
                 "tbl_ps tbl_sb tbl_out0 tbl_out1 firsts_ready firsts_dram firstrow_in rows_ready rows_in "
                 "cls_ready cls_ps pair_ready pair_out srcp_out efp_out pad_out "
                 "loop_ready rhi_done rres_done rmid_done rsplit relw6_in rec_ready info_dram info_in deg_T plan_col plan_ps "
                 "win_ready win_hot win_ps "
                 "passed tab_ready wraw_in wsplit win_iota loop_n loop_t "
                 "bst_ready blk_in tg0 tg1 l0_math n2_ready th_ready hnorm hnorm_out h2_ready h2_out "
                 "bst1_ready src_in ef_in idx_ready hi_done res_done mid_done lo_done valid_in "
                 "hg0 hg1 h_free efT_ps efT_sb w_ready w_free d_ready c_ready "
                 "sub_done exp_done q_ready q_free sum_done sum_read fin out_done init").split()
        m = {n: sem("s_" + n) for n in names}
        tgath, hgath = (m["tg0"], m["tg1"]), (m["hg0"], m["hg1"])

        block = ctx.enter_context(nc.Block())

        def bc(v, n):
            return v.unsqueeze(len(v.shape)).to_broadcast(list(v.shape) + [n])

        def steps(eng):
            n = eng.value_load(npair[0:1, 0:1], min_val=C // 2, max_val=NW // 2 - 2)
            return n, (2 * n + 2) // WCH + 1

        def window(eng, k):
            v = eng.value_load(tabgn[:, ds(k, 1)], min_val=0, max_val=C * NHW + NHW - 1)
            return v // NHW, v % NHW + 1

        def blocks(nh):
            return (nh + 1) // 2

        @block.sync
        def _(sp):
            sp.dma_start(rec[:, :, 0:D], x.rearrange("(p c) d -> p c d", p=PN)).then_inc(m["x_in"], 16)
            sp.dma_start(dst_sb, dst.rearrange("(p e) -> p e", p=PN)).then_inc(m["dst_in"], 16)
            sp.wait_ge(m["wzero"], 1)
            sp.dma_start(relW[0:D, 0:RO].rearrange("i (r o) -> i r o", o=D), relw.rearrange("r i o -> i r o")).then_inc(m["relw_in"], 16)
            sp.dma_start(relW[D:D + 1, 0:RO], relemb.rearrange("(a r) o -> a (r o)", a=1)).then_inc(m["relw_in"], 16)
            sp.dma_start(relW[0:D, RO:RO + D], loopw).then_inc(m["relw_in"], 16)
            sp.dma_start(src_sb, src.rearrange("(p e) -> p e", p=PN)).then_inc(m["edges_in"], 16)
            sp.dma_start(et_sb, etype.rearrange("(p e) -> p e", p=PN)).then_inc(m["edges_in"], 16)
            sp.dma_start(srcp_d[0:E].rearrange("(a b) -> a b", b=250), src.rearrange("(a b) -> a b", b=250)).then_inc(m["srcp_out"], 16)
            for j, (wt, bias) in enumerate(((wattn, battn), (wmsg, bmsg))):
                sp.dma_start(wraw[0:D, j * IO:(j + 1) * IO], wt).then_inc(m["wraw_in"], 16)
                sp.dma_start(wraw[D:D + 1, j * IO:(j + 1) * IO], bias.rearrange("(a c) -> a c", a=1)).then_inc(m["wraw_in"], 16)
            sp.wait_ge(m["rsplit"], 1)
            for j, part in enumerate((0, 1, 2, 0, 1, 0)):
                sp.dma_start(relW6[j * (D + 1):(j + 1) * (D + 1), :], rparts[:, part, :]).then_inc(m["relw6_in"], 16)
            sp.wait_ge(m["pads_ready"], 1)
            sp.dma_start(srcp_d[E:E + S].rearrange("(a b) -> a b", a=1), padrow[:, 0:S].bitcast(I32)).then_inc(m["pad_out"], 16)
            sp.dma_start(pairp_d[E:E + S].rearrange("(a b) -> a b", a=1), padrow[:, 0:S].bitcast(I32)).then_inc(m["pad_out"], 16)
            sp.dma_start(efp_d[E * D:(E + S) * D].rearrange("(a b) -> a b", a=1), padrow).then_inc(m["pad_out"], 16)
            sp.dma_start(h2_d[N:N + 1, :], pad1[:]).then_inc(m["pad_out"], 16)
            rows = table_d.rearrange("(p c r) d -> p c (r d)", p=PN, c=C)
            with sp.Fori(0, C // 2) as t:
                for j in range(2):
                    sp.wait_ge(m["tbl_sb"], t * 8 + (4 * j + 4 + 2))
                    for a, b in ((0, 112), (112, PN)):
                        sp.dma_start(rows[a:b, ds(2 * t + j, 1), :].rearrange("p a n -> p (a n)"),
                                     tbl[a:b, j, :]).then_inc(m[f"tbl_out{j}"], 16)
            sp.dma_start(efp_d[0:E * D].rearrange("(a b) -> a b", b=1375),
                         efeat.rearrange("e d -> (e d)").rearrange("(a b) -> a b", b=1375)).then_inc(m["efp_out"], 16)
            sp.wait_ge(m["wsplit"], 1)
            for j, part in enumerate((0, 1, 2, 0, 1, 0)):
                sp.dma_start(wst[j * D:(j + 1) * D, :], wparts[0:D, part, :]).then_inc(m["wts_in"], 16)
            for part in range(3):
                sp.dma_start(wst[6 * D + part:6 * D + part + 1, :], wparts[D:D + 1, part, :]).then_inc(m["wts_in"], 16)
            sp.dma_start(wst[KE - 1:KE, :], urow[:]).then_inc(m["wts_in"], 16)
            sp.wait_ge(m["efp_out"], 16)
            sp.wait_ge(m["wts_in"], 16 * 10)

        @block.gpsimd
        def _(pool):
            pool.memset(ident[:], 0.0).then_inc(m["init"], 1)
            pool.memset(tri[:], 1.0).then_inc(m["init"], 1)
            pool.iota(nodei[:], [[1, C + 1]], base=0, channel_multiplier=C).then_inc(m["init"], 1)
            pool.iota(iotai[:], [[1, NV]], base=0, channel_multiplier=0).then_inc(m["init"], 1)
            pool.wait_ge(m["init"], 4)
            pool.affine_select(out=ident[:], in_=ident[:], compare_op=ALU.not_equal, fill=1.0, base=0,
                               pattern=[[-1, 128]], channel_multiplier=1).then_inc(m["const"], 1)
            pool.affine_select(out=tri[:], in_=tri[:], compare_op=ALU.is_ge, fill=0.0, base=0,
                               pattern=[[1, PN]], channel_multiplier=-1).then_inc(m["const"], 1)
            pool.wait_ge(m["firsts_ready"], 1)
            pool.dma_start(first_d.rearrange("(p c) -> p c", p=PN), firsts[:]).then_inc(m["firsts_dram"], 16)
            pool.wait_ge(m["firsts_dram"], 16)
            pool.dma_start(firstrow, first_d.rearrange("(a c) -> a c", a=1).to_broadcast([PN, NROW])).then_inc(m["firstrow_in"], 16)
            pool.wait_ge(m["rows_ready"], 1)
            for c in range(C + 1):
                pool.indirect_dma_start(out=dstblk[:, c, :], out_offset=None, in_=dst.rearrange("(r w) -> r w", w=ROW),
                                        in_offset=bass.IndirectOffsetOnAxis(ap=rowi[:, c:c + 1].bitcast(U32), axis=0)).then_inc(m["rows_in"], 16)
            pool.wait_ge(m["pair_ready"], 1)
            pool.dma_start(pairp_d[0:E].rearrange("(p e) -> p e", p=PN), pair_sb).then_inc(m["pair_out"], 16)
            pool.wait_ge(m["rec_ready"], 1)
            for c in range(C):
                pool.indirect_dma_start(out=info_d, out_offset=bass.IndirectOffsetOnAxis(ap=ranki[:, c:c + 1].bitcast(U32), axis=0),
                                        in_=rec[:, c, :], in_offset=None).then_inc(m["info_dram"], 16)
            pool.iota(winint, [[1, WCH]], base=0, channel_multiplier=0).then_inc(m["win_iota"], 1)
            pool.wait_ge(m["info_dram"], 16 * C)
            for a in (0, C // 2):
                pool.dma_start(info[:, a:a + C // 2, :],
                               info_d[a * PN:(a + C // 2) * PN, :].rearrange("(g p) w -> p g w", p=PN)).then_inc(m["info_in"], 16)

            pool.wait_ge(m["win_ready"], 16)
            pairs = pool.value_load(npair[0:1, 0:1], min_val=C // 2, max_val=NW // 2 - 2)
            pool.wait_ge(m["tbl_out0"], 2 * 16 * (C // 2))
            pool.wait_ge(m["tbl_out1"], 2 * 16 * (C // 2))
            pool.wait_ge(m["pair_out"], 16)
            pool.wait_ge(m["pad_out"], 16 * 4)
            cum = [pool.alloc_register("cumP0"), pool.alloc_register("cumP1")]
            for r in cum:
                pool.reg_mov(r, 0)

            def pair_block(w, q):
                pool.wait_ge(m["bst_ready"], w + 1)
                pool.sem_inc(m["passed"], 1)
                pool.indirect_dma_start(out=blkidx[:, q, :], out_offset=None, in_=pairp_d.rearrange("(e a) -> e a", a=1),
                                        in_offset=bass.IndirectOffsetOnAxis(ap=bst[:, q:q + 1].bitcast(U32), axis=0)).then_inc(m["blk_in"], 16)

            def gather(rows, idx, q, b, n, done):
                for s in range(b * n, (b + 1) * n):
                    pool.indirect_dma_start(out=gath[:, q, s, :], out_offset=None, in_=rows,
                                            in_offset=bass.IndirectOffsetOnAxis(ap=idx[:, q, s:s + 1].bitcast(U32), axis=0)).then_inc(done[q], 16)

            pair_block(0, 0)
            with pool.Fori(0, pairs) as i:
                for q in range(2):
                    k = 2 * i + q
                    _, nh = window(pool, k)
                    pool.wait_ge(m["blk_in"], 16 * k + 16)
                    pool.wait_ge(m["l0_math"], k + 1)
                    pool.sem_inc(m["passed"], 1)
                    for b in range(MINH):
                        gather(table_d, blkidx, q, b, HALF, tgath)
                    if q:
                        pool.wait_ge(tgath[0], pool.snap(cum[0]) * (16 * HALF))
                        pool.sem_inc(m["passed"], 1)
                    else:
                        with pool.If(i > 0):
                            pool.wait_ge(tgath[1], pool.snap(cum[1]) * (16 * HALF))
                            pool.sem_inc(m["passed"], 1)
                    pair_block(k + 1, 1 - q)
                    for b in range(MINH, NHW):
                        with pool.If(nh > b):
                            gather(table_d, blkidx, q, b, HALF, tgath)
                    pool.reg_add(cum[q], cum[q], nh)
            pool.wait_ge(m["blk_in"], pairs * 32 + 16)
            pool.sem_inc(m["passed"], 1)
            pool.wait_ge(m["srcp_out"], 16)
            pool.wait_ge(m["efp_out"], 16)

            def edge_block(w, q, first=False):
                pool.wait_ge(m["bst1_ready"], w + 1)
                if not first:
                    pool.wait_ge(m["res_done"], w)
                pool.sem_inc(m["passed"], 1)
                off = bass.IndirectOffsetOnAxis(ap=bst[:, q:q + 1].bitcast(U32), axis=0)
                pool.indirect_dma_start(out=blkidx[:, q, :], out_offset=None, in_=srcp_d.rearrange("(e a) -> e a", a=1),
                                        in_offset=off).then_inc(m["src_in"], 16)
                pool.indirect_dma_start(out=efraw[:, 0, 0:S * D], out_offset=None, in_=efp_d.rearrange("(e d) -> e d", d=D),
                                        in_offset=off).then_inc(m["ef_in"], 16)

            edge_block(0, 0, first=True)
            pool.wait_ge(m["h2_ready"], 1)
            for c in range(C):
                pool.indirect_dma_start(out=h2_d, out_offset=bass.IndirectOffsetOnAxis(ap=nidx[:, c:c + 1].bitcast(U32), axis=0),
                                        in_=h2[:, c, :], in_offset=None).then_inc(m["h2_out"], 16)
            def residue(w):
                pool.wait_ge(m["hi_done"], w + 1)
                nc.gpsimd.tensor_tensor(efres, efin, efs[:, :, HI:HI + D], ALU.subtract).then_inc(m["res_done"], 1)

            def last_part(w):
                pool.wait_ge(m["mid_done"], w + 1)
                nc.gpsimd.tensor_tensor(efs[:, :, LO:LO + D], efres, efs[:, :, MID:MID + D], ALU.subtract).then_inc(m["lo_done"], 1)

            sent = pool.alloc_register("sent")
            pool.reg_mov(sent, 0)

            def scatter(q):
                w = pool.snap(sent)
                pool.wait_ge(m["fin"], w + 1)
                pool.sem_inc(m["passed"], 1)
                with pool.If(w > 0):
                    pool.wait_ge(m["out_done"], w * 16)
                    pool.sem_inc(m["passed"], 1)
                pool.indirect_dma_start(out=out, out_offset=bass.IndirectOffsetOnAxis(ap=oidx[:, q:q + 1].bitcast(U32), axis=0),
                                        in_=orow[:, q, :], in_offset=None, bounds_check=N - 1, oob_is_err=False).then_inc(m["out_done"], 16)
                pool.reg_add(sent, sent, 1)

            pool.wait_ge(m["h2_out"], 16 * C)
            with pool.Fori(0, pairs) as i:
                for q in range(2):
                    k = 2 * i + q
                    _, nh = window(pool, k)
                    pool.wait_ge(m["idx_ready"], k + 1)
                    pool.wait_ge(m["h_free"], k + 1)
                    pool.sem_inc(m["passed"], 1)
                    residue(k)
                    edge_block(k + 1, 1 - q)
                    for b in range(MINH):
                        gather(h2_d, hidx, q, b, HALF, hgath)
                        if b == MINH // 2 - 1:
                            last_part(k)
                    for b in range(MINH, NHW):
                        with pool.If(nh > b):
                            gather(h2_d, hidx, q, b, HALF, hgath)
                    with pool.If(i > 0):
                        scatter(q)
            residue(2 * pairs)
            last_part(2 * pairs)
            for q in range(2):
                scatter(q)
            pool.wait_ge(m["out_done"], pairs * 32)

        @block.tensor
        def _(pe):
            pe.wait_ge(m["const"], 2)
            pe.wait_ge(m["htan_ready"], 1)
            for t in range((C + 7) // 8):
                if t >= 3:
                    pe.wait_ge(m["hT_sb"], t - 2)
                for j in range(min(8, C - 8 * t)):
                    last = nc.tensor.transpose(psTb[0:KT, t % 3, j, 0:PN], htan6[:, 8 * t + j, :, :].rearrange("p j k -> p (j k)"),
                                               identb[0:PN, 0:PN])
                last.then_inc(m["hT_ps"], 1)
            pe.wait_ge(m["relw6_in"], 16 * 6)
            pe.wait_ge(m["hT_sb"], (C + 7) // 8)

            def table_steps(t0, t1):
                with pe.Fori(t0, t1) as t:
                    for j in range(2):
                        for h in range(4):
                            u = 4 * j + h
                            pe.wait_ge(m["tbl_sb"], t * 8 + (u + 1))
                            for a in range(2):
                                c0 = (2 * h + a) * PIECE
                                n = PIECE + (D if h == 3 and a else 0)
                                last = nc.tensor.matmul(psW[0:PN, u % 2, 512 * a:512 * a + n],
                                                        hT6[:, ds(2 * t + j, 1), 0:PN].rearrange("k a n -> k (a n)"),
                                                        relW6[:, c0:c0 + n], start=True, stop=True)
                            last.then_inc(m["tbl_ps"], 1)

            table_steps(0, TSTEP)
            pe.wait_ge(m["cls_ready"], 1)
            nc.tensor.matmul(psS[0:PN, 0:NV], ones[:], ncls, start=True, stop=True)
            nc.tensor.matmul(psS[0:PN, NV:2 * NV], tri[:], ncls, start=True, stop=True).then_inc(m["cls_ps"], 1)
            table_steps(TSTEP, C // 2)
            pe.wait_ge(m["info_in"], 32)
            nc.tensor.transpose(psT[0:C, 0, 0:PN], info[:, 0:C, 2 * D + 1], ident[0:PN, 0:PN]).then_inc(m["deg_T"], 1)
            pe.wait_ge(m["plan_col"], 1)
            nc.tensor.matmul(psT[0:C, 4, 0:1], tri[0:C, 0:C], col[:, 2:3], start=True, stop=True)
            nc.tensor.matmul(psT[0:PN, 8, 0:1], ones[0:C, :], col[:, 2:3], start=True, stop=True).then_inc(m["plan_ps"], 1)
            pe.wait_ge(m["plan_col"], 2)
            pairs, nstep = steps(pe)
            with pe.Fori(0, nstep) as t:
                pe.wait_ge(m["win_hot"], t + 1)
                for j, rhs in ((0, winhot), (1, winhot), (2, winrel)):
                    last = nc.tensor.matmul(psT[0:PN, 4 * j:4 * j + 4, :].rearrange("p a n -> p (a n)"), lhs[:, j, :],
                                            rhs, start=True, stop=True)
                last.then_inc(m["win_ps"], 1)

            pe.wait_ge(m["win_ready"], 16)
            pe.wait_ge(m["wts_in"], 16 * 10)
            cumb, nhp = pe.alloc_register("cumBp"), pe.alloc_register("nhPrev")
            pe.reg_mov(cumb, 0)
            pe.reg_mov(nhp, 0)

            def transposes(w):
                pe.wait_ge(m["lo_done"], w + 1)
                pe.wait_ge(m["valid_in"], w + 1)
                for t in range(S // 8):
                    pe.wait_ge(m["efT_sb"], w * (S // 8) + (t + 1))
                    for j in range(8):
                        last = nc.tensor.transpose(psTb[0:KE, t % 3, j, 0:PN], efs[:, 8 * t + j, :], identb[0:PN, 0:PN])
                    last.then_inc(m["efT_ps"], 1)

            def weights(c0, q, h, at0):
                pe.wait_ge(m["w_free"], at0 + (h + 1))
                for j in range(HALF):
                    last = nc.tensor.matmul(psW[0:PN, h % 2, j * IO:(j + 1) * IO], efT[:, q, h * HALF + j, 0:PN],
                                            wst[:, c0:c0 + IO], start=True, stop=True)
                last.then_inc(m["w_ready"], 1)

            def exp_sums(q, h):
                for s in range(h * HALF, (h + 1) * HALF):
                    nc.tensor.matmul(psS[0:PN, 0:IO], ident[0:PN, 0:PN], score[:, q, s, :], start=False, stop=False)

            def prod_sums(h):
                for s in range(HALF):
                    c0 = (h % (2 * RING) * HALF + s) * IO
                    nc.tensor.matmul(psS[0:PN, IO:2 * IO], ident[0:PN, 0:PN], prod[:, c0:c0 + IO], start=False, stop=False)

            def close_sums():
                nc.tensor.matmul(psS[0:PN, :], zero[:, 0:PN], zero[:], start=False, stop=True).then_inc(m["sum_done"], 1)

            transposes(0)
            with pe.Fori(0, pairs) as i:
                for q in range(2):
                    k = 2 * i + q
                    _, nh = window(pe, k)
                    nb = blocks(nh)
                    tb, prev = pe.snap(cumb), pe.snap(nhp)
                    pe.wait_ge(m["efT_sb"], k * (S // 8) + (S // 8 + 3))
                    for h in range(NHW):
                        if h < MINH:
                            weights(0, q, h, tb * 4)
                        else:
                            with pe.If(nh > h):
                                weights(0, q, h, tb * 4)
                        with pe.If(prev > h):
                            exp_sums(1 - q, h)
                    with pe.If(prev > 0):
                        close_sums()
                    for h in range(2):
                        weights(IO, q, h, tb * 4 + nb * 2)
                    transposes(k + 1)
                    pe.wait_ge(m["sum_read"], k + 1)
                    nc.tensor.matmul(psS[0:PN, :], zero[:, 0:PN], zero[:], start=True, stop=False)
                    for b in range(NBW):
                        for h in range(2 * b + 2, min(2 * b + 4, NHW)):
                            if h < MINH:
                                weights(IO, q, h, tb * 4 + nb * 2)
                            else:
                                with pe.If(nh > h):
                                    weights(IO, q, h, tb * 4 + nb * 2)
                        with pe.If(nb > b):
                            pe.wait_ge(m["q_ready"], tb + (b + 1))
                            prod_sums(2 * b)
                            with pe.If(nh > 2 * b + 1):
                                prod_sums(2 * b + 1)
                            nc.tensor.matmul(psS[0:PN, IO:2 * IO], zero[:, 0:PN], zero[:, 0:IO], start=False,
                                             stop=False).then_inc(m["q_free"], 1)
                    pe.reg_add(cumb, cumb, nb)
                    pe.reg_mov(nhp, nh)
            prev = pe.snap(nhp)
            for h in range(NHW):
                with pe.If(prev > h):
                    exp_sums(1, h)
            close_sums()

        @block.scalar
        def _(act):
            act.wait_ge(m["var_ready"], 1)
            nc.scalar.activation(nrm[:, 1, :], nrm[:, 0, :], ACT.Sqrt).then_inc(m["std_ready"], 1)
            act.wait_ge(m["var_ready"], 2)
            nc.scalar.activation(nrm[:, 1, :], nrm[:, 0, :], ACT.Sqrt).then_inc(m["std_ready"], 1)
            act.wait_ge(m["relw_in"], 16 * 3)
            nc.scalar.copy(rparts[:, 0, :], relW).then_inc(m["rhi_done"], 1)
            act.wait_ge(m["rres_done"], 1)
            nc.scalar.copy(rparts[:, 1, :], relW).then_inc(m["rmid_done"], 1)
            for t in range((C + 7) // 8):
                n = min(8, C - 8 * t)
                act.wait_ge(m["hT_ps"], t + 1)
                nc.scalar.copy(hT6[:, 8 * t:8 * t + n, 0:PN], psTb[0:KT, t % 3, 0:n, 0:PN]).then_inc(m["hT_sb"], 1)
            with act.Fori(0, C // 2) as t:
                for j in range(2):
                    with act.If(t > 0):
                        act.wait_ge(m[f"tbl_out{j}"], t * 32)
                        act.sem_inc(m["passed"], 1)
                    for h in range(4):
                        u = 4 * j + h
                        act.wait_ge(m["tbl_ps"], t * 8 + (u + 1))
                        if h == 3:
                            nc.scalar.copy(rec[:, ds(2 * t + j, 1), D:2 * D].rearrange("p a d -> p (a d)"),
                                           psW[0:PN, u % 2, 512 + PIECE:512 + PIECE + D]).then_inc(m["loop_ready"], 1)
                        nc.scalar.copy(tbl[:, j, 2 * h * PIECE:(2 * h + 2) * PIECE].rearrange("p (a n) -> p a n", a=2),
                                       psW[0:PN, u % 2, :].rearrange("p (a n) -> p a n", a=2)[:, :, 0:PIECE]).then_inc(m["tbl_sb"], 1)
            act.wait_ge(m["loop_n"], 1)
            nc.scalar.activation(nrm[:, 3, :], nrm[:, 2, :], ACT.Sqrt).then_inc(m["loop_t"], 1)
            act.wait_ge(m["loop_t"], 1)
            nc.scalar.activation(nrm[:, 4, :], nrm[:, 3, :], ACT.Tanh, scale=SQC).then_inc(m["loop_t"], 1)

            act.wait_ge(m["tab_ready"], 1)
            act.dma_start(tabgn, tabtmp).then_inc(m["win_ready"], 16)
            act.wait_ge(m["win_ready"], 16)
            pairs = act.value_load(npair[0:1, 0:1], min_val=C // 2, max_val=NW // 2 - 2)
            with act.Fori(0, pairs) as i:
                for q in range(2):
                    k = 2 * i + q
                    act.wait_ge(m["n2_ready"], k + 1)
                    nc.scalar.activation(sl[:, 2, :], sl[:, 1, :], ACT.Sqrt)
                    nc.scalar.drain()
                    nc.scalar.activation(sl[:, 3, :], sl[:, 2, :], ACT.Tanh, scale=SQC).then_inc(m["th_ready"], 1)
            act.wait_ge(m["hnorm"], 1)
            nc.scalar.activation(nrm[:, 1, :], nrm[:, 0, :], ACT.Sqrt).then_inc(m["hnorm_out"], 1)
            act.wait_ge(m["hnorm"], 2)
            nc.scalar.activation(nrm[:, 1, :], nrm[:, 0, :], ACT.Sqrt).then_inc(m["hnorm_out"], 1)
            act.wait_ge(m["hnorm"], 3)
            nc.scalar.activation(nrm[:, 1, :], nrm[:, 0, :], ACT.Sqrt).then_inc(m["hnorm_out"], 1)

            cumb = act.alloc_register("cumBa")
            act.reg_mov(cumb, 0)

            def split(w):
                act.wait_ge(m["ef_in"], 16 * w + 16)
                nc.scalar.copy(efs[:, :, HI:MID].rearrange("p s (t d) -> p s t d", d=D),
                               efin.unsqueeze(2).to_broadcast([PN, S, 3, D])).then_inc(m["hi_done"], 1)
                act.wait_ge(m["res_done"], w + 1)
                nc.scalar.copy(efs[:, :, MID:LO].rearrange("p s (t d) -> p s t d", d=D),
                               efres.unsqueeze(2).to_broadcast([PN, S, 2, D])).then_inc(m["mid_done"], 1)

            def copies(w, q):
                for t in range(S // 8):
                    act.wait_ge(m["efT_ps"], w * (S // 8) + (t + 1))
                    nc.scalar.copy(efT[:, q, 8 * t:8 * t + 8, 0:PN], psTb[0:KE, t % 3, :, 0:PN]).then_inc(m["efT_sb"], 1)

            split(0)
            copies(0, 0)
            with act.Fori(0, pairs) as i:
                for q in range(2):
                    k = 2 * i + q
                    split(k + 1)
                    copies(k + 1, 1 - q)
                    _, nh = window(act, k)
                    nb = blocks(nh)
                    tb = act.snap(cumb)
                    act.wait_ge(m["d_ready"], k + 1)
                    nc.scalar.activation(cfac[:, q, :], diff[:, q, :], ACT.Exp).then_inc(m["c_ready"], 1)
                    with act.Fori(0, nh // 2) as b:
                        act.wait_ge(m["sub_done"], tb + b + 1)
                        v = score[:, q, ds(b * BLK, BLK), :]
                        nc.scalar.activation(v, v, ACT.Exp).then_inc(m["exp_done"], 1)
                    with act.If(nh % 2 > 0):
                        act.wait_ge(m["sub_done"], tb + nb)
                        v = score[:, q, ds((nh - 1) // 2 * BLK, HALF), :]
                        nc.scalar.activation(v, v, ACT.Exp).then_inc(m["exp_done"], 1)
                    act.reg_add(cumb, cumb, nb)

        @block.vector
        def _(dve):
            V = nc.vector
            for name, n in (("tbl_sb", 2), ("l0_math", 2), ("h_free", 2), ("efT_sb", 3), ("w_free", 2), ("q_free", RING),
                            ("sum_read", 1)):
                dve.sem_inc(m[name], n)
            V.memset(relW[:, RO:RO + D], 0.0)
            V.drain().then_inc(m["wzero"], 1)
            V.memset(urow[:, 0:IO], -BIG)
            V.memset(urow[:, IO:2 * IO], 0.0)
            V.memset(pad1[:], 1.0)
            V.memset(gath[:], 0.0)
            V.memset(zero[:], 0.0)
            V.memset(ones[:], 1.0)
            V.memset(info[:], 0.0)
            V.memset(npad[:], float(N))
            V.memset(lamsum[:], 0.0)
            V.memset(xnew[:], 0.0)
            V.memset(htan6[:, :, 0:3, D:D + 1], 1.0)
            V.memset(htan6[:, :, 3:6, D:D + 1], 0.0)
            V.drain().then_inc(m["pads_ready"], 1)

            def row_sum(o, i):
                V.tensor_reduce(o, i, AX.X, ALU.add)
                V.drain()

            def tt(o, a, b, op):
                V.tensor_tensor(o, a, b, op)
                V.drain()

            def ts(o, a, s1, s2, op0, op1=None):
                if op1 is None:
                    V.tensor_scalar(o, a, s1, None, op0)
                else:
                    V.tensor_scalar(o, a, s1, s2, op0, op1)
                V.drain()

            def norm_relu(o, i, t0, to_act, from_act, n):
                row_sum(nrm[:, 2, :], i)
                ts(nrm[:, 2, :], nrm[:, 2, :], 1.0 / D, None, ALU.mult)
                tt(t0, i, bc(nrm[:, 2, :], D), ALU.subtract)
                tt(o, t0, t0, ALU.mult)
                row_sum(nrm[:, 2, :], o)
                V.tensor_scalar(nrm[:, 0, :], nrm[:, 2, :], 1.0 / D, LN_EPS, ALU.mult, ALU.add).then_inc(to_act, 1)
                dve.wait_ge(from_act, n)
                V.reciprocal(nrm[:, 2, :], nrm[:, 1, :])
                V.drain()
                tt(t0, t0, bc(nrm[:, 2, :], D), ALU.mult)
                ts(o, t0, 0.0, None, ALU.max)

            dve.wait_ge(m["dst_in"], 16)
            V.tensor_copy(firsts[:], dst_sb.rearrange("p (r w) -> p r w", w=ROW)[:, :, 0]).then_inc(m["firsts_ready"], 1)
            dve.wait_ge(m["x_in"], 16)
            h, t0, t1 = tmp(0), tmp(1), tmp(2)
            norm_relu(h, rec[:, :, 0:D], t0, m["var_ready"], m["std_ready"], 1)
            tt(t0, h, h, ALU.mult)
            row_sum(nrm[:, 2, :], t0)
            V.tensor_scalar(nrm[:, 0, :], nrm[:, 2, :], MIN_NORM, None, ALU.max).then_inc(m["var_ready"], 1)
            dve.wait_ge(m["std_ready"], 2)
            z, z2, acc = nrm[:, 2, :], nrm[:, 3, :], nrm[:, 4, :]
            ts(z, nrm[:, 1, :], SQC, 1.0 - BALL, ALU.mult, ALU.min)
            tt(z2, z, z, ALU.mult)
            ts(acc, z2, 1.0 / 23, 1.0 / 21, ALU.mult, ALU.add)
            for n in range(19, 0, -2):
                tt(acc, acc, z2, ALU.mult)
                ts(acc, acc, 1.0 / n, None, ALU.add)
            tt(t0, h, bc(acc, D), ALU.mult)
            V.tensor_copy(htan6[:, :, 0:3, 0:D], t0.unsqueeze(2).to_broadcast([PN, C, 3, D]))
            V.drain()
            tt(t0, t0, htan6[:, :, 0, 0:D], ALU.subtract)
            V.tensor_copy(htan6[:, :, 3:5, 0:D], t0.unsqueeze(2).to_broadcast([PN, C, 2, D]))
            V.drain()
            dve.wait_ge(m["const"], 2)
            V.tensor_copy(identb[:], ident[:])
            V.tensor_tensor(htan6[:, :, 5, 0:D], t0, htan6[:, :, 3, 0:D], ALU.subtract)
            V.drain().then_inc(m["htan_ready"], 1)
            dve.wait_ge(m["rhi_done"], 1)
            V.tensor_tensor(relW, relW, rparts[:, 0, :], ALU.subtract)
            V.drain().then_inc(m["rres_done"], 1)
            dve.wait_ge(m["edges_in"], 32)
            V.scalar_tensor_tensor(pair_sb, src_sb, float(R), et_sb, ALU.mult, ALU.add).then_inc(m["pair_ready"], 1)
            dve.wait_ge(m["rmid_done"], 1)
            V.tensor_tensor(rparts[:, 2, :], relW, rparts[:, 1, :], ALU.subtract)
            V.drain().then_inc(m["rsplit"], 1)

            V.tensor_copy(nodeid[:], nodei[:])
            V.tensor_copy(iotaf[:], iotai[:])
            V.drain()
            dve.wait_ge(m["firstrow_in"], 16)
            for c in range(C + 1):
                V.tensor_scalar(junk, firstrow, nodeid[:, c:c + 1], 0.0, ALU.is_lt, ALU.add,
                                accum_out=cnt[:, c:c + 1])
                V.drain()
            ts(cnt[:], cnt[:], -1.0, 0.0, ALU.add, ALU.max)
            V.tensor_copy(rowi[:], cnt[:]).then_inc(m["rows_ready"], 1)
            dve.wait_ge(m["hT_ps"], (C + 7) // 8)
            dve.wait_ge(m["rows_in"], 16 * (C + 1))
            tt(less, dstblk, bc(nodeid[:], ROW), ALU.is_lt)
            row_sum(start0[:], less)
            V.scalar_tensor_tensor(start0[:], cnt[:], float(ROW), start0[:], ALU.mult, ALU.add)
            V.drain()
            tt(rec[:, :, 2 * D + 1], start0[:, 1:C + 1], start0[:, 0:C], ALU.subtract)
            V.tensor_copy(rec[:, :, 2 * D], start0[:, 0:C])
            V.tensor_copy(rec[:, :, 2 * D + 2], nodeid[:, 0:C])
            V.memset(rec[:, :, 2 * D + 3:2 * D + 4], 0.0)
            ts(key[:], rec[:, :, 2 * D + 1], -1.0, float(NV - 1), ALU.mult, ALU.add)
            ts(key[:], key[:], 0.0, None, ALU.max)
            tt(onehot, bc(iotaf[:], C), key[:].unsqueeze(1).to_broadcast([PN, NV, C]), ALU.is_equal)
            V.tensor_reduce(ncls, onehot, AX.X, ALU.add)
            V.drain().then_inc(m["cls_ready"], 1)
            flat = onehot.rearrange("p v c -> p (v c)")
            V.tensor_tensor_scan(count.rearrange("p v c -> p (v c)"), flat, flat, 0.0, ALU.add, ALU.max)
            dve.wait_ge(m["cls_ps"], 1)
            V.tensor_copy(total_cls, psS[0:PN, 0:NV])
            V.drain()
            V.tensor_tensor_scan(base, total_cls, total_cls, 0.0, ALU.add, ALU.max)
            V.drain()
            tt(base, base, total_cls, ALU.subtract)
            tt(base, base, psS[0:PN, NV:2 * NV], ALU.add)
            V.scalar_tensor_tensor(base, count[:, :, C - 1], -1.0, base, ALU.mult, ALU.add)
            V.drain()
            ts(base, base, -1.0, None, ALU.add)
            tt(count, count, bc(base, C), ALU.add)
            tt(count, count, onehot, ALU.mult)
            row_sum(rank[:], count.rearrange("p v c -> p c v"))
            V.tensor_copy(ranki[:], rank[:])
            dve.wait_ge(m["loop_ready"], C)
            lp = rec[:, :, D:2 * D]
            tt(t0, lp, lp, ALU.mult)
            row_sum(nrm[:, 2, :], t0)
            V.tensor_scalar(nrm[:, 2, :], nrm[:, 2, :], MIN_NORM, None, ALU.max)
            V.drain().then_inc(m["loop_n"], 1)
            dve.wait_ge(m["loop_t"], 2)
            ts(nrm[:, 3, :], nrm[:, 3, :], SQC, None, ALU.mult)
            V.reciprocal(nrm[:, 5, :], nrm[:, 3, :])
            V.drain()
            tt(nrm[:, 4, :], nrm[:, 4, :], nrm[:, 5, :], ALU.mult)
            tt(lp, lp, bc(nrm[:, 4, :], D), ALU.mult)
            V.drain().then_inc(m["rec_ready"], 1)

            dve.wait_ge(m["wraw_in"], 16 * 4)
            V.tensor_copy(wparts[:, 0, :], wraw)
            V.drain()
            tt(wres, wraw, wparts[:, 0, :], ALU.subtract)
            V.tensor_copy(wparts[:, 1, :], wres)
            V.drain()
            V.tensor_tensor(wparts[:, 2, :], wres, wparts[:, 1, :], ALU.subtract)
            V.drain().then_inc(m["wsplit"], 1)
            dve.wait_ge(m["relw6_in"], 16 * 6)
            V.memset(tabtmp, 0)
            V.memset(numer, 0.0)
            dve.wait_ge(m["deg_T"], 1)
            V.tensor_reduce(col[:, 0:1], psT[0:C, 0, 0:PN], AX.X, ALU.max)
            V.drain()
            MAGIC = 8388608.0

            def ceil_div(o, i, n):
                ts(o, i, 1.0, None, ALU.max)
                ts(o, o, (n - 1) / 2.0, 1.0 / n, ALU.add, ALU.mult)
                ts(o, o, MAGIC, None, ALU.add)
                ts(o, o, -MAGIC, None, ALU.add)

            ceil_div(col[:, 1:2], col[:, 0:1], HALF)
            ceil_div(col[:, 2:3], col[:, 1:2], NHW)
            V.drain().then_inc(m["plan_col"], 1)
            dve.wait_ge(m["plan_ps"], 1)
            V.tensor_copy(col[:, 3:4], psT[0:C, 4, 0:1])
            V.tensor_copy(npairf[:], psT[0:PN, 8, 0:1])
            V.drain()
            tt(col[:, 4:5], col[:, 3:4], col[:, 2:3], ALU.subtract)
            ts(npairf[:], npairf[:], 0.5, 0.25, ALU.mult, ALU.add)
            ts(npairf[:], npairf[:], MAGIC, None, ALU.add)
            ts(npairf[:], npairf[:], -MAGIC, None, ALU.add)
            V.tensor_copy(npair[:], npairf[:])
            dve.wait_ge(m["win_iota"], 1)
            V.tensor_copy(winpos, winint)
            V.tensor_copy(nidx[:, 0:C], info[:, 0:C, 2 * D + 2])
            V.tensor_copy(nidx[:, C:C + 1], npad[:])
            ts(col[:, 5:6], nodeid[0:C, 0:1], 1.0 / C, None, ALU.mult)
            ts(col[:, 5:6], col[:, 5:6], MAGIC, None, ALU.add)
            ts(col[:, 5:6], col[:, 5:6], -MAGIC, None, ALU.add)
            ts(col[:, 5:6], col[:, 5:6], -float(C), None, ALU.add)
            for j, cc in ((0, 5), (1, 1)):
                ts(lhs[:, j, :], ones[0:C, :], col[:, cc:cc + 1], None, ALU.mult)
            V.tensor_copy(lhs[:, 2, :], ones[0:C, :])
            V.drain().then_inc(m["plan_col"], 1)
            pairs, nstep = steps(dve)
            with dve.Fori(0, nstep) as t:
                V.tensor_scalar(winrel, winpos, col[:, 3:4], None, ALU.is_ge)
                V.drain()
                V.scalar_tensor_tensor(winhot, winpos, col[:, 4:5], winrel, ALU.is_ge, ALU.subtract)
                V.drain()
                V.scalar_tensor_tensor(winrel, winpos, col[:, 4:5], winhot, ALU.subtract, ALU.mult)
                V.tensor_scalar(winpos, winpos, float(WCH), None, ALU.add)
                V.drain().then_inc(m["win_hot"], 1)
                dve.wait_ge(m["win_ps"], t + 1)
                pg, pn, pr = (psT[0:PN, 4 * j:4 * j + 4, :].rearrange("p a n -> p (a n)") for j in range(3))
                V.tensor_copy(tabs[0:PN, ds(WCH * t, WCH)], pr)
                V.tensor_copy(wv[:, 0, :], pr)
                V.drain()
                V.scalar_tensor_tensor(wv[:, 0, :], wv[:, 0, :], -float(NHW), pn, ALU.mult, ALU.add)
                V.tensor_scalar(wv[:, 1, :], pg, float(NHW), float(NHW * C - 1), ALU.mult, ALU.add)
                V.drain()
                ts(wv[:, 0, :], wv[:, 0, :], float(NHW), float(MINH), ALU.min, ALU.max)
                tt(tabtmp[:, ds(WCH * t, WCH)], wv[0:1, 1, :], wv[0:1, 0, :], ALU.add)
            V.drain().then_inc(m["tab_ready"], 1)
            dve.wait_ge(m["win_ready"], 16)

            start = info[:, :, 2 * D]
            deg = info[:, :, 2 * D + 1]

            def window_start(w, q, done):
                g, _ = window(dve, w)
                n = tabs[0:PN, ds(w, 1)]
                V.scalar_tensor_tensor(bstf[:, q:q + 1], n, float(S), start[:, ds(g, 1)], ALU.mult, ALU.add)
                V.scalar_tensor_tensor(rem[:, q:q + 1], n, -float(S), deg[:, ds(g, 1)], ALU.mult, ALU.add)
                V.tensor_scalar(keep[:, q:q + 1], n, 1.0, None, ALU.min)
                V.drain()
                V.tensor_scalar(keepbig[:, q:q + 1], keep[:, q:q + 1], -1.0, 2.0 * BIG, ALU.add, ALU.mult)
                V.tensor_scalar(bst[:, q:q + 1], bstf[:, q:q + 1], float(E), None, ALU.min)
                V.drain().then_inc(done, 1)

            cum = [dve.alloc_register("cumV0"), dve.alloc_register("cumV1")]
            for r in cum:
                dve.reg_mov(r, 0)
            window_start(0, 0, m["bst_ready"])
            with dve.Fori(0, pairs) as i:
                for q in range(2):
                    k = 2 * i + q
                    G = gath[:, q, :, :]
                    g, nh = window(dve, k)
                    dve.reg_add(cum[q], cum[q], nh)
                    V.tensor_scalar(valid[:, q, :], iotaf[:, 0:S], rem[:, q:q + 1], None, ALU.is_lt)
                    if q:
                        dve.wait_ge(m["blk_in"], 16 * k)
                        dve.sem_inc(m["passed"], 1)
                    else:
                        with dve.If(i > 0):
                            dve.wait_ge(m["blk_in"], 16 * k)
                            dve.sem_inc(m["passed"], 1)
                    window_start(k + 1, 1 - q, m["bst_ready"])
                    dve.wait_ge(tgath[q], dve.snap(cum[q]) * (16 * HALF))
                    tt(sq, G, G, ALU.mult)
                    row_sum(sl[:, 0, :], sq)
                    V.tensor_scalar(sl[:, 1, :], sl[:, 0, :], MIN_NORM, None, ALU.max).then_inc(m["n2_ready"], 1)
                    dve.wait_ge(m["th_ready"], k + 1)
                    ts(sl[:, 2, :], sl[:, 2, :], SQC, None, ALU.mult)
                    V.reciprocal(sl[:, 4, :], sl[:, 2, :])
                    V.drain()
                    tt(sl[:, 3, :], sl[:, 3, :], sl[:, 4, :], ALU.mult)
                    tt(sl[:, 4, :], sl[:, 3, :], sl[:, 3, :], ALU.mult)
                    tt(sl[:, 4, :], sl[:, 4, :], sl[:, 0, :], ALU.mult)
                    ts(sl[:, 4, :], sl[:, 4, :], -CURV, 1.0, ALU.mult, ALU.add)
                    ts(sl[:, 4, :], sl[:, 4, :], EPS, 0.5, ALU.add, ALU.mult)
                    V.reciprocal(sl[:, 5, :], sl[:, 4, :])
                    V.drain()
                    tt(sl[:, 5, :], sl[:, 5, :], valid[:, q, :], ALU.mult)
                    row_sum(lsum[:], sl[:, 5, :])
                    tt(sl[:, 3, :], sl[:, 3, :], sl[:, 5, :], ALU.mult)
                    V.tensor_tensor(sq, G, bc(sl[:, 3, :], D), ALU.mult)
                    V.drain().then_inc(m["l0_math"], 1)
                    row_sum(nsum[:], sq.rearrange("p s d -> p d s"))
                    V.tensor_tensor(numer[:, ds(g, 1), :].rearrange("p a d -> p (a d)"),
                                    numer[:, ds(g, 1), :].rearrange("p a d -> p (a d)"), nsum[:], ALU.add)
                    V.tensor_tensor(lamsum[:, ds(g, 1)], lamsum[:, ds(g, 1)], lsum[:], ALU.add)
                    V.drain()

            dve.wait_ge(m["blk_in"], pairs * 32 + 16)
            dve.sem_inc(m["passed"], 1)
            window_start(0, 0, m["bst1_ready"])
            window_start(1, 1, m["bst1_ready"])

            A, B, T = tmp(0), tmp(1), tmp(2)
            X0, Y = info[:, 0:C, 0:D], info[:, 0:C, D:2 * D]
            n0, n1, n2, n3, n4, n5 = (nrm[:, j, :] for j in (2, 3, 4, 5, 6, 7))
            V.tensor_scalar(nrm[:, 0, :], deg[:, 0:C], 1.0, None, ALU.max).then_inc(m["hnorm"], 1)
            dve.wait_ge(m["hnorm_out"], 1)
            V.reciprocal(n0, nrm[:, 1, :])
            V.drain()
            tt(n1, n0, deg[:, 0:C], ALU.mult)
            ts(n1, n1, EPS, None, ALU.add)
            V.reciprocal(n2, n1)
            V.drain()
            tt(n0, n0, n2, ALU.mult)
            tt(n1, n0, lamsum[:, 0:C], ALU.mult)
            ts(n1, n1, EPS, None, ALU.add)
            V.reciprocal(n2, n1)
            V.drain()
            tt(n0, n0, n2, ALU.mult)
            tt(A, numer[:, 0:C, :], bc(n0, D), ALU.mult)
            tt(T, A, A, ALU.mult)
            row_sum(n0, T)
            V.tensor_scalar(nrm[:, 0, :], n0, MIN_NORM, None, ALU.max).then_inc(m["hnorm"], 1)
            dve.wait_ge(m["hnorm_out"], 2)
            V.reciprocal(n1, nrm[:, 1, :])
            V.drain()
            ts(n1, n1, (1.0 - BALL) / SQC, 1.0, ALU.mult, ALU.min)
            tt(A, A, bc(n1, D), ALU.mult)
            tt(T, A, A, ALU.mult)
            row_sum(n0, T)
            tt(T, Y, Y, ALU.mult)
            row_sum(n1, T)
            tt(T, A, Y, ALU.mult)
            row_sum(n2, T)
            ts(n3, n2, 2.0 * CURV, 1.0, ALU.mult, ALU.add)
            tt(n4, n0, n1, ALU.mult)
            V.scalar_tensor_tensor(n4, n4, CURV * CURV, n3, ALU.mult, ALU.add)
            V.scalar_tensor_tensor(n3, n1, CURV, n3, ALU.mult, ALU.add)
            V.drain()
            ts(n4, n4, MIN_NORM, None, ALU.max)
            V.reciprocal(n5, n4)
            ts(n0, n0, -CURV, 1.0, ALU.mult, ALU.add)
            tt(T, A, bc(n3, D), ALU.mult)
            tt(B, Y, bc(n0, D), ALU.mult)
            tt(T, T, B, ALU.add)
            tt(T, T, bc(n5, D), ALU.mult)
            tt(xnew[:, 0:C, :], X0, T, ALU.add)
            norm_relu(h2, xnew[:, 0:C, :], tmp(3), m["hnorm"], m["hnorm_out"], 3)
            V.drain().then_inc(m["h2_ready"], 1)

            V.memset(mnew, 0.0)
            V.memset(total, 0.0)
            V.drain()
            sent = dve.alloc_register("sentV")
            dve.reg_mov(sent, 0)
            cumb, cumh = dve.alloc_register("cumBv"), dve.alloc_register("cumHv")
            dve.reg_mov(cumb, 0)
            dve.reg_mov(cumh, 0)
            for r in cum:
                dve.reg_mov(r, 0)

            def edge_ids(w, q):
                dve.wait_ge(m["src_in"], 16 * w + 16)
                ts(valid[:, q, :], iotaf[:, 0:S], rem[:, q:q + 1], None, ALU.is_lt)
                V.scalar_tensor_tensor(valid2[:], blkidx[:, q, :], -float(N), valid[:, q, :], ALU.add, ALU.mult)
                V.drain()
                V.tensor_scalar(hidx[:, q, :], valid2[:], float(N), None, ALU.add)
                V.drain().then_inc(m["idx_ready"], 1)

            def edge_valid(w, q):
                V.tensor_copy(efs[:, :, 6 * D:6 * D + 3], bc(valid[:, q, :], 3))
                V.tensor_scalar(efs[:, :, KE - 1], valid[:, q, :], -1.0, 1.0, ALU.mult, ALU.add)
                V.drain().then_inc(m["valid_in"], 1)

            def finish(q, n):
                dve.wait_ge(m["c_ready"], n)
                tt(total, total, cfac[:, q, :].unsqueeze(1).to_broadcast([PN, 2, IO]), ALU.mult)
                dve.wait_ge(m["sum_done"], n)
                V.tensor_tensor(total, total, psS[0:PN, :].rearrange("p (a c) -> p a c", a=2), ALU.add)
                V.drain().then_inc(m["sum_read"], 1)
                V.reciprocal(ratio, total[:, 0, :])
                V.drain()
                tt(ratio, ratio, total[:, 1, :], ALU.mult)
                row_sum(ft[:], ratio.rearrange("p (i o) -> p o i", o=D))
                V.scalar_tensor_tensor(orow[:, q, :], ft[:], gx[:, q, D:D + 1], gx[:, q, 0:D], ALU.mult, ALU.add)
                V.tensor_copy(oidx[:, q:q + 1], gid[:, q:q + 1])
                V.drain().then_inc(m["fin"], 1)

            def row_free():
                dve.reg_add(sent, sent, 16)
                dve.wait_ge(m["out_done"], dve.snap(sent))
                dve.sem_inc(m["passed"], 1)

            edge_ids(0, 0)
            edge_valid(0, 0)
            with dve.Fori(0, pairs) as i:
                for q in range(2):
                    k = 2 * i + q
                    edge_ids(k + 1, 1 - q)
                    g, nh = window(dve, k)
                    nb = blocks(nh)
                    last, odd = (nh - 1) // 2, nh % 2
                    tb, th = dve.snap(cumb), dve.snap(cumh)
                    dve.reg_add(cum[q], cum[q], nh)
                    V.tensor_scalar(mold, mnew[:, 1 - q, :], keep[:, q:q + 1], keepbig[:, q:q + 1], ALU.mult, ALU.add)
                    V.tensor_copy(gx[:, q, 0:D], xnew[:, ds(g, 1), :].rearrange("p a d -> p (a d)"))
                    V.tensor_scalar(gx[:, q, D:D + 1], deg[:, ds(g, 1)], 1.0, None, ALU.min)
                    V.tensor_copy(gid[:, q:q + 1], nidx[:, ds(g, 1)])
                    V.drain()
                    window_start(k + 2, q, m["bst1_ready"])
                    dve.wait_ge(hgath[q], dve.snap(cum[q]) * (16 * HALF))

                    def times_h(dst_ap, b, s, at0, free=1):
                        dve.wait_ge(m["w_ready"], at0 + (s + 1))
                        hb = gath[:, q, ds(b * BLK + HALF * s, HALF), :]
                        V.tensor_tensor(dst_ap.rearrange("p s (i o) -> p s i o", o=D),
                                        psW[0:PN, s, 0:HALF * IO].rearrange("p (s i o) -> p s i o", i=D, o=D),
                                        bc(hb, D), ALU.mult).then_inc(m["w_free"], free)

                    def scores(b, halves=2):
                        for s in range(halves):
                            times_h(score[:, q, ds(b * BLK + HALF * s, HALF), :], b, s, th * 2 + b * 2, 3 - halves)
                        V.drain()

                    scores(0)
                    scores(1)
                    V.tensor_tensor(macc, score[:, q, 0:BLK, :], score[:, q, BLK:2 * BLK, :], ALU.max)
                    edge_valid(k + 1, 1 - q)
                    with dve.Fori(2, nh // 2) as b:
                        scores(b)
                        V.tensor_tensor(macc, macc, score[:, q, ds(b * BLK, BLK), :], ALU.max)
                    with dve.If(odd > 0):
                        scores(last, 1)
                        V.tensor_tensor(macc[:, 0:HALF, :], macc[:, 0:HALF, :], score[:, q, ds(last * BLK, HALF), :], ALU.max)
                    V.drain()
                    V.tensor_reduce(mred, macc.rearrange("p s c -> p c s"), AX.X, ALU.max)
                    V.drain()
                    tt(mnew[:, q, :], mred, mold, ALU.max)
                    V.tensor_tensor(diff[:, q, :], mold, mnew[:, q, :], ALU.subtract).then_inc(m["d_ready"], 1)

                    if q:
                        with dve.If(i > 0):
                            row_free()
                        finish(0, k)
                    else:
                        with dve.If(i > 1):
                            row_free()
                        with dve.If(i > 0):
                            finish(1, k)

                    def messages(b, halves=2):
                        n = halves * HALF
                        blk = score[:, q, ds(b * BLK, n), :]
                        V.tensor_tensor(blk, blk, mnew[:, q, :].unsqueeze(1).to_broadcast([PN, n, IO]),
                                        ALU.subtract).then_inc(m["sub_done"], 1)
                        dve.wait_ge(m["q_free"], tb + b + 1)
                        par = (b % RING) * (BLK * IO)
                        for s in range(halves):
                            times_h(prod[:, ds(par + HALF * s * IO, HALF * IO)].rearrange("p (s c) -> p s c", c=IO), b, s,
                                    th * 2 + nh + b * 2, 3 - halves)
                        V.drain()
                        dve.wait_ge(m["exp_done"], tb + b + 1)
                        pr = prod[:, ds(par, n * IO)]
                        V.tensor_tensor(pr, pr, blk.rearrange("p s c -> p (s c)"), ALU.mult).then_inc(m["q_ready"], 1)

                    with dve.Fori(0, nh // 2) as b:
                        messages(b)
                    with dve.If(odd > 0):
                        messages(last, 1)
                    V.drain().then_inc(m["h_free"], 1)
                    dve.reg_add(cumb, cumb, nb)
                    dve.reg_add(cumh, cumh, nh)
            row_free()
            finish(1, pairs * 2)


_INS = ["x", "src", "dst", "edge_attr_16", "edge_type_230", "L0_gnn_rel_weight", "L0_gnn_loop_weight", "L0_gnn_rel_emb",
        "L1_gnn_W_msg", "L1_gnn_b_msg", "L1_gnn_W_attn", "L1_gnn_b_attn"]


def kernel(**inputs):
    import numpy as _np
    import concourse.bacc as _bacc
    from concourse.bass_utils import run_bass_kernel_spmd as _run

    nc = _bacc.Bacc("TRN2", target_bir_lowering=False, num_devices=1)
    arrays, args = {}, []
    for name in _INS:
        a = _np.ascontiguousarray(inputs[name])
        arrays[f"in_{name}"] = a
        args.append(nc.dram_tensor(f"in_{name}", a.shape, mybir.dt.from_np(a.dtype), kind="ExternalInput").ap())
    out = nc.dram_tensor("out_0", (N, D), F32, kind="ExternalOutput").ap()
    scratch = [nc.dram_tensor(n, s, t, kind="Internal").ap() for n, s, t in (
        ("table", (N * R, D), F32), ("srcp", (E + S,), I32), ("pairp", (E + S,), I32), ("efp", ((E + S) * D,), F32),
        ("h2_dram", (N + 1, D), F32), ("first_dram", (NROW,), F32), ("info_dram", (N, INFO), F32))]
    build(nc, *args, out, scratch)
    r = _run(nc, [arrays], core_ids=[0])
    return r.results[0]["out_0"]
```
